# Optimizing a Trainium2 kernel written in Bass

```python
import numpy as np
import jax
import jax.numpy as jnp

def _softmax(x, axis=-1):
    return jax.nn.softmax(x, axis=axis)

def _gelu(x):
    return jax.nn.gelu(x, approximate=True)

def _silu(x):
    return jax.nn.silu(x)

def _sigmoid(x):
    return jax.nn.sigmoid(x)

def _layernorm(x, axis=-1, eps=1e-05):
    m = jnp.mean(x, axis=axis, keepdims=True)
    v = jnp.var(x, axis=axis, keepdims=True)
    return (x - m) / jnp.sqrt(v + eps)

def _scatter_add(tgt, idx, src, axis=0):
    return tgt.at[idx].add(src)

def _segment_sum(src, seg, n):
    return jax.ops.segment_sum(src, seg, n)
kernel_name = 'mk_audio_tower_d1_tok_audfeat2048_r4_40c506'

def setup_inputs(seed: int=0):
    np.random.seed(seed)
    _w = jnp.asarray

    def _rec_inputs():
        import jax
        import jax.numpy as jnp
        _rk = jax.random.key(seed)
        x = -0.000520686 + 1.00062 * jax.random.normal(jax.random.fold_in(_rk, 1), (64, 4096, 1), jnp.float32)
        return x
    x = _rec_inputs()

    def _L0_tok_setup():
        import jax, jax.numpy as jnp
        import numpy as np
        PATCH_LEN = 128
        D_MODEL = 512
        BATCH = 128
        SEQ_LEN = 4096
        FEATURES = 1
        key = jax.random.key(seed)
        k1, k2, k3 = jax.random.split(key, 3)
        x = jax.random.normal(k1, (BATCH, SEQ_LEN, FEATURES), dtype=jnp.float32)
        W = jax.random.normal(k2, (D_MODEL, PATCH_LEN), dtype=jnp.float32) * (1.0 / np.sqrt(PATCH_LEN))
        b = jax.random.normal(k3, (D_MODEL,), dtype=jnp.float32) * 0.01
        return {'x': x, 'W': W, 'b': b}
    _L0_tok_all = _L0_tok_setup()
    _L0_tok_in = {k: v for k, v in _L0_tok_all.items() if k in ('W', 'b')}
    del _L0_tok_all

    def _L0_attn_setup():
        import jax, jax.numpy as jnp
        import numpy as np
        E = 512
        H = 3
        key = jax.random.key(seed)
        ks = jax.random.split(key, 6)
        B, N = (4, 512)
        x = jax.random.normal(ks[0], (B, N, E), dtype=jnp.float32)
        Wq = jax.random.normal(ks[1], (H, E, E), dtype=jnp.float32) * 0.02
        Wk = jax.random.normal(ks[2], (H, E, E), dtype=jnp.float32) * 0.02
        Wv = jax.random.normal(ks[3], (H, E, E), dtype=jnp.float32) * 0.02
        fc_w = jax.random.normal(ks[4], (E, E), dtype=jnp.float32) * 0.02
        fc_b = jax.random.normal(ks[5], (E,), dtype=jnp.float32) * 0.02
        return {'x': x, 'Wq': Wq, 'Wk': Wk, 'Wv': Wv, 'fc_w': fc_w, 'fc_b': fc_b}
    _L0_attn_all = _L0_attn_setup()
    _L0_attn_in = {k: v for k, v in _L0_attn_all.items() if k in ('Wq', 'Wk', 'Wv', 'fc_w', 'fc_b')}
    del _L0_attn_all

    def _L0_ffn_setup():
        import jax, jax.numpy as jnp
        import numpy as np
        BS, SLEN, DIM, HID, E, TOPK = (4, 512, 512, 448, 8, 2)
        key = jax.random.key(seed)
        ks = jax.random.split(key, 9)
        s = 0.02
        return {'x': jax.random.normal(ks[0], (BS, SLEN, DIM), jnp.float32), 'gate_w': jax.random.normal(ks[1], (DIM, E), jnp.float32) * s, 'w1': jax.random.normal(ks[2], (E, DIM, HID), jnp.float32) * s, 'w2': jax.random.normal(ks[3], (E, HID, DIM), jnp.float32) * s, 'w3': jax.random.normal(ks[4], (E, DIM, HID), jnp.float32) * s, 'sw1': jax.random.normal(ks[5], (DIM, HID), jnp.float32) * s, 'sw2': jax.random.normal(ks[6], (HID, DIM), jnp.float32) * s, 'sw3': jax.random.normal(ks[7], (DIM, HID), jnp.float32) * s, 'expert_bias': jnp.zeros((E,), jnp.float32)}
    _L0_ffn_all = _L0_ffn_setup()
    _L0_ffn_in = {k: v for k, v in _L0_ffn_all.items() if k in ('gate_w', 'w1', 'w2', 'w3', 'sw1', 'sw2', 'sw3', 'expert_bias')}
    del _L0_ffn_all
    return {'x': x, 'L0_tok_W': _L0_tok_in['W'], 'L0_tok_b': _L0_tok_in['b'], 'L0_attn_Wq': _L0_attn_in['Wq'], 'L0_attn_Wk': _L0_attn_in['Wk'], 'L0_attn_Wv': _L0_attn_in['Wv'], 'L0_attn_fc_w': _L0_attn_in['fc_w'], 'L0_attn_fc_b': _L0_attn_in['fc_b'], 'L0_ffn_gate_w': _L0_ffn_in['gate_w'], 'L0_ffn_w1': _L0_ffn_in['w1'], 'L0_ffn_w2': _L0_ffn_in['w2'], 'L0_ffn_w3': _L0_ffn_in['w3'], 'L0_ffn_sw1': _L0_ffn_in['sw1'], 'L0_ffn_sw2': _L0_ffn_in['sw2'], 'L0_ffn_sw3': _L0_ffn_in['sw3'], 'L0_ffn_expert_bias': _L0_ffn_in['expert_bias']}

def reference(x, L0_tok_W, L0_tok_b, L0_attn_Wq, L0_attn_Wk, L0_attn_Wv, L0_attn_fc_w, L0_attn_fc_b, L0_ffn_gate_w, L0_ffn_w1, L0_ffn_w2, L0_ffn_w3, L0_ffn_sw1, L0_ffn_sw2, L0_ffn_sw3, L0_ffn_expert_bias):
    import jax
    import jax.numpy as jnp

    def _L0_tok_ref(x, W, b):
        import jax, jax.numpy as jnp
        import numpy as np
        PATCH_LEN = 128
        D_MODEL = 512
        BATCH = 128
        SEQ_LEN = 4096
        FEATURES = 1
        B, S, F = x.shape
        P = PATCH_LEN
        stride = P // 2
        starts = jnp.arange(0, S - P + 1, stride)
        idx = starts[:, None] + jnp.arange(P)
        patches = x[:, idx, :].reshape(B, starts.shape[0], P * F)
        patches = patches[:, :, :P]
        return jnp.einsum('bnp,dp->bnd', patches, W) + b

    def _L0_attn_ref(x, Wq, Wk, Wv, fc_w, fc_b):
        import jax, jax.numpy as jnp
        import numpy as np
        E = 512
        H = 3
        Q = jnp.einsum('bne,hde->hbnd', x, Wq)
        K = jnp.einsum('bne,hde->hbnd', x, Wk)
        V = jnp.einsum('bne,hde->hbnd', x, Wv)
        scale = 1.0 / jnp.sqrt(jnp.float32(E))
        scores = jnp.einsum('hbnd,hbmd->hbnm', Q, K) * scale
        w = jax.nn.softmax(scores, axis=2)
        attn = jnp.einsum('hbnm,hbmd->hbnd', w, V)
        mean = jnp.mean(attn, axis=0)
        return mean @ fc_w.T + fc_b

    def _L0_ffn_ref(x, gate_w, w1, w2, w3, sw1, sw2, sw3, expert_bias):
        import jax, jax.numpy as jnp
        import numpy as np
        BS, SLEN, DIM, HID, E, TOPK = (4, 512, 512, 448, 8, 2)
        bs, slen, dim = x.shape
        T = bs * slen
        xf = x.reshape(T, dim)
        scores = jax.nn.softmax((xf @ gate_w).astype(jnp.float32), axis=-1)
        _, sel = jax.lax.top_k(scores + expert_bias[None, :], TOPK)
        top_scores = jnp.take_along_axis(scores, sel, axis=1)
        flat_sel = sel.reshape(-1)
        counts = jnp.bincount(flat_sel, length=E).astype(jnp.int32)
        order = jnp.argsort(flat_sel, stable=True)
        top_scores_sorted = top_scores.reshape(-1)[order]
        token_idx = order // TOPK
        routed_in = xf[token_idx] * top_scores_sorted[:, None]
        h = jax.nn.silu(jax.lax.ragged_dot(routed_in, w1, counts)) * jax.lax.ragged_dot(routed_in, w3, counts)
        routed_out = jax.lax.ragged_dot(h, w2, counts)
        out = jax.nn.silu(xf @ sw1) * (xf @ sw3) @ sw2
        out = out.at[token_idx].add(routed_out)
        return out.reshape(bs, slen, dim)
    h = _L0_tok_ref(x, L0_tok_W, L0_tok_b)
    h = h + _L0_attn_ref(_layernorm(h, axis=-1), L0_attn_Wq, L0_attn_Wk, L0_attn_Wv, L0_attn_fc_w, L0_attn_fc_b)
    h = h + _L0_ffn_ref(_layernorm(h, axis=-1), L0_ffn_gate_w, L0_ffn_w1, L0_ffn_w2, L0_ffn_w3, L0_ffn_sw1, L0_ffn_sw2, L0_ffn_sw3, L0_ffn_expert_bias)
    return h

_drawn_inputs = setup_inputs


def setup_inputs(seed=0):
    import zlib

    import numpy as np

    out = dict(_drawn_inputs(seed))
    spreads = {'L0_ffn_expert_bias': (0.0, 0.8)}
    factors = {'L0_tok_b': 5.73,
     'L0_attn_Wq': 8.0,
     'L0_attn_Wk': 8.0,
     'L0_attn_Wv': 3.783,
     'L0_attn_fc_w': 3.675,
     'L0_attn_fc_b': 2.814,
     'L0_ffn_gate_w': 8.0,
     'L0_ffn_w1': 8.0,
     'L0_ffn_w2': 8.0,
     'L0_ffn_w3': 8.0,
     'L0_ffn_sw1': 8.0,
     'L0_ffn_sw2': 8.0,
     'L0_ffn_sw3': 8.0}
    for name, (base, spread) in spreads.items():
        noise = np.random.default_rng([zlib.crc32(name.encode()), seed]).standard_normal(out[name].shape)
        drawn = base * np.exp(spread * noise) if base else spread * noise
        out[name] = jnp.asarray(drawn.astype(out[name].dtype))
    for name, factor in factors.items():
        out[name] = (out[name] * factor).astype(out[name].dtype)
    return out
```

```python
import concourse.bass as bass
from concourse import mybir
from contextlib import ExitStack

BATCH, SAMPLES = 64, 4096
PATCH, STRIDE = 128, 64
SEQ = (SAMPLES - PATCH) // STRIDE + 1
PAD_SEQ = 64
DIM, HEADS, HID, EXPERTS, TOPK = 512, 3, 448, 8, 2
P, LOG_P = 128, 7
TOKENS = BATCH * PAD_SEQ
TILES = TOKENS // P
KT = DIM // P
HB = HID // KT
SLOT_TILES = (TOKENS * TOPK + EXPERTS * (P - 1)) // P
EPS = 1e-5
A1 = PATCH + 1
W_WORDS = 2 * KT * HID + KT * DIM


def audio_tower(nc, x, tokWT, tokW, tokb, WqT, WkT, WvT, fcT, fcb, gate_w, w1, w2, w3, sw1, sw2, sw3, ebias, out):
    f32, u32 = mybir.dt.float32, mybir.dt.uint32
    ALU, ACT, AX = mybir.AluOpType, mybir.ActivationFunctionType, mybir.AxisListType
    ctx = ExitStack()
    with ctx:
        def sb(name, shape, dt=f32):
            return ctx.enter_context(nc.sbuf_tensor(name, shape, dt))

        def sem(name):
            return ctx.enter_context(nc.semaphore(name))

        xn_dram = nc.dram_tensor("xn_rows", [TOKENS + P, DIM], f32, kind="Internal").ap()

        experts = sb("experts", [P, EXPERTS * W_WORDS])
        place = [0]

        def words(n, *dims, parts=P):
            a = place[0]
            place[0] += n
            assert place[0] <= EXPERTS * W_WORDS
            v = experts[0:parts, a:a + n]
            if len(dims) == 2:
                v = v.rearrange("p (a b) -> p a b", a=dims[0])
            if len(dims) == 3:
                v = v.rearrange("p (a b c) -> p a b c", a=dims[0], b=dims[1])
            return v

        qkvT = words(3 * HEADS * KT * DIM, 3 * HEADS, KT, DIM)
        fcT_sb = words(KT * DIM, KT, DIM)
        qkvA = words(3 * HEADS * KT * A1, 3 * HEADS, KT, A1)
        A_T = words(KT * A1, KT, A1)
        EARLY = 5
        assert place[0] <= EARLY * W_WORDS - 2 * A1
        A_mean = words(A1)
        bc2 = words(KT)

        place[0] = EARLY * W_WORDS
        sw_sb = words(W_WORDS)
        sw1_sb = sw_sb[:, 0:KT * HID].rearrange("p (k h) -> p k h", k=KT)
        sw3_sb = sw_sb[:, KT * HID:2 * KT * HID].rearrange("p (k h) -> p k h", k=KT)
        sw2_sb = sw_sb[0:HB, 2 * KT * HID:].rearrange("p (k d) -> p k d", k=KT)
        F = words(HEADS * DIM, HEADS, DIM)
        tokWT_sb = words(DIM)
        tail = words(DIM, parts=HEADS + 2)
        f128 = words(HEADS * DIM, HEADS, DIM, parts=1)
        GT = words(HEADS * P, HEADS, P)
        g_row = words(HEADS)
        g_col = words(HEADS)
        g00 = words(HEADS, parts=1)
        S = words(A1)
        s00e = words(1)
        gw_sb = words(KT * EXPERTS, KT, EXPERTS)
        patches = words(A1)
        dots = words(A1)
        PT = words(P)
        U = words(HEADS * P, HEADS, P)
        varsum, rstd, rscale, rmask = words(1), words(1), words(1), words(1)
        diag = words(P)
        c_sb = words(HEADS)
        Rbc = words(PAD_SEQ)
        s1 = words(HEADS * SEQ, HEADS, SEQ)
        s2 = words(HEADS * SEQ, HEADS, SEQ)
        mx, nmx, esum, winv = words(HEADS), words(HEADS), words(HEADS), words(HEADS)
        ex = words(HEADS * SEQ, HEADS, SEQ)
        mixw = words(HEADS * P, HEADS, P)
        YT = words(HEADS * P, HEADS, P)
        y0 = words(P, parts=HEADS + 2)
        h2 = words(DIM)
        stats, aggr, var2, rstd2 = words(6), words(2), words(1), words(1)
        neg_half = words(1)
        xn = words(DIM)
        xnT = words(DIM, KT, P)
        sig = words(HID)
        act = words(HID)
        hT = words(KT * P, KT, P)
        acc = words(DIM)
        onehot_h = words(HEADS * HEADS, HEADS, HEADS)
        mask = words(1)
        ones1 = words(PAD_SEQ)
        ones_row = words(P, parts=1)

        ident = sb("ident", [P, P])
        ones = sb("ones", [P, P])
        logits = sb("logits", [P, TILES, EXPERTS])
        slot_idx = sb("slot_idx", [P, SLOT_TILES], u32)
        slot_score = sb("slot_score", [P, SLOT_TILES])
        tile_expert = sb("tile_expert", [1, SLOT_TILES], u32)

        g_idx = sb("g_idx", [P, 1], u32)
        s_idx = sb("s_idx", [P, 1], u32)
        score = sb("score", [P, 1])
        xg = sb("xg", [P, DIM])
        xgT = sb("xgT", [P, KT, P])
        rgate = sb("rgate", [P, HID])
        ract = sb("ract", [P, HID])
        rhT = sb("rhT", [P, KT, P])
        y_sb = sb("y_sb", [P, DIM])

        place[0] = EARLY * W_WORDS
        TE = TILES * EXPERTS

        def te():
            return words(TE, TILES, EXPERTS)
        z, prob, choice, iota_e, eq, oh1, oh2, M, incl, pos = (te() for _ in range(10))
        tmp = te()
        rmx, rsum, v1, i1, v2, i2 = (words(TILES) for _ in range(6))
        C = TOPK * TILES
        pk, low, hi, val, prob_k = (words(C, TOPK, TILES) for _ in range(5))
        bias_bc = words(EXPERTS)
        rconst_done = words(1)
        totals, ntiles, ends, starts = (words(EXPERTS) for _ in range(4))
        int_e = words(EXPERTS).bitcast(u32)
        int_k, int_low = (words(C).bitcast(u32).rearrange("p (a b) -> p a b", a=TOPK) for _ in range(2))
        tri = words(P)
        iota_p = words(P)
        iota_s = words(SLOT_TILES)
        spare_row = words(1)
        tok_id = words(TILES)
        CG = 4
        lowhot = [words(CG * P, CG, P) for _ in range(2)]
        hihot = [words(CG * SLOT_TILES, CG, SLOT_TILES) for _ in range(2)]
        hival = [words(CG * 2 * SLOT_TILES, CG, 2 * SLOT_TILES) for _ in range(2)]
        te_cmp = words(SLOT_TILES * EXPERTS, SLOT_TILES, EXPERTS, parts=1)
        te_sum = words(SLOT_TILES, parts=1)

        bank = [ctx.enter_context(nc.psum_tensor(f"bank{i}", [P, DIM], f32)) for i in range(8)]

        s_tok, s_qkv, s_fc = sem("s_tok"), sem("s_qkv"), sem("s_fc")
        s_bload, s_patch, s_tail = sem("s_bload"), sem("s_patch"), sem("s_tail")
        s_expert = sem("s_expert")
        s_zrow, s_xnst, s_accst = sem("s_zrow"), sem("s_xnst"), sem("s_accst")
        s_gather, s_scatter = sem("s_gather"), sem("s_scatter")
        s_issue = sem("s_issue")
        s_const = sem("s_const")
        s_pc = sem("s_pc")
        s_dv = sem("s_dv")
        s_mean, s_cen, s_sps = sem("s_mean"), sem("s_cen"), sem("s_sps")
        s_bc2, s_ssb, s_wa, s_wae, s_gf, s_gfe = (sem(n) for n in ("s_bc2", "s_ssb", "s_wa", "s_wae", "s_gf", "s_gfe"))
        s_folded = sem("s_folded")
        names = ("t_vare t_var2 t_sigd t_pt t_ptsb t_sps t_cps t_ups t_var t_rstd t_diag t_usb t_csb t_rps t_rbc t_scps t_s1 t_s2 t_mx t_nmx "
                 "t_exp t_rm t_esi t_winv t_mixw t_yps t_ysb t_h2ps t_stats t_aggr t_rstd2 t_xn t_h2sb t_xtps t_xtsb "
                 "t_gps t_lg t_h1ps t_h3ps t_exps t_sig t_sact t_act t_htps t_htsb t_ops t_acc").split()
        T = {n: sem(n) for n in names}
        r_exp, r_ez, r_M, r_rank, r_oh, r_ohused, r_list, r_done = (
            sem(n) for n in ("r_exp", "r_ez", "r_M", "r_rank", "r_oh", "r_ohused", "r_list", "r_done"))
        names = "e_idx e_sidx e_xps e_xsb e_h1ps e_h3ps e_gate e_act e_htps e_htsb e_yps e_ysb".split()
        R = {n: sem(n) for n in names}

        block = ctx.enter_context(nc.Block())

        w1_d = w1.rearrange("e (k p) h -> e p k h", p=P)
        w3_d = w3.rearrange("e (k p) h -> e p k h", p=P)
        w2_d = w2.rearrange("e (k p) d -> e p k d", p=HB)
        out_t = out[0:TOKENS, :].rearrange("(t p) d -> t p d", p=P)
        xn_t = xn_dram[0:TOKENS, :].rearrange("(t p) d -> t p d", p=P)

        def expert_view(e):
            o = e * W_WORDS
            return (experts[:, o:o + KT * HID].rearrange("p (k h) -> p k h", k=KT),
                    experts[:, o + KT * HID:o + 2 * KT * HID].rearrange("p (k h) -> p k h", k=KT),
                    experts[0:HB, o + 2 * KT * HID:o + W_WORDS].rearrange("p (k d) -> p k d", k=KT))

        def patch_rows(row, n):
            return bass.AP(tensor=x.tensor, offset=row * STRIDE, ap=[[STRIDE, n], [1, PATCH]])

        @block.sync
        def _(sp):
            sp.dma_start(A_T[:, :, 0:PATCH], tokW.rearrange("(k p) q -> p k q", p=P)).then_inc(s_tok, 16)
            with nc.allow_non_contiguous_dma(reason="512 words of bias, one in a channel's partition"):
                sp.dma_start(A_T[:, :, PATCH:A1], tokb.rearrange("(k p a) -> p k a", p=P, a=1)).then_inc(s_tok, 16)
            for m, w in enumerate((WqT, WkT, WvT)):
                for h in range(HEADS):
                    sp.dma_start(qkvT[:, m * HEADS + h], w[h].rearrange("(k p) d -> p k d", p=P)).then_inc(s_qkv, 16)
            sp.dma_start(fcT_sb[:], fcT.rearrange("(k p) o -> p k o", p=P)).then_inc(s_fc, 16)
            sp.dma_start(tokWT_sb[:], tokWT[:, :]).then_inc(s_bload, 16)
            sp.dma_start(tail[HEADS:HEADS + 1, :], tokb.rearrange("(a d) -> a d", a=1)).then_inc(s_bload, 16)
            sp.dma_start(tail[HEADS + 1:HEADS + 2, :], fcb.rearrange("(a d) -> a d", a=1)).then_inc(s_bload, 16)
            sp.dma_start(gw_sb[:], gate_w.rearrange("(k p) e -> p k e", p=P)).then_inc(s_bload, 16)
            sp.dma_start(sw1_sb, sw1.rearrange("(k p) h -> p k h", p=P)).then_inc(s_bload, 16)
            sp.dma_start(sw3_sb, sw3.rearrange("(k p) h -> p k h", p=P)).then_inc(s_bload, 16)
            sp.dma_start(sw2_sb, sw2.rearrange("(k p) d -> p k d", p=HB)).then_inc(s_bload, 16)
            sp.wait_ge(s_folded, 1)
            for h in range(HEADS):
                sp.dma_start(tail[h:h + 1, :], f128[0:1, h, :]).then_inc(s_tail, 16)
            for e in range(EARLY):
                for dst, src in zip(expert_view(e), (w1_d[e], w3_d[e], w2_d[e])):
                    sp.dma_start(dst, src).then_inc(s_expert, 16)
                sp.wait_ge(s_expert, 48 * (e + 1))
            sp.wait_ge(r_done, 1)
            for e in range(EARLY, EXPERTS):
                for dst, src in zip(expert_view(e), (w1_d[e], w3_d[e], w2_d[e])):
                    sp.dma_start(dst, src).then_inc(s_expert, 16)
                sp.wait_ge(s_expert, 48 * (e + 1))

        @block.gpsimd
        def _(pool):
            n = [0]

            def link(ins):
                n[0] += 1
                ins.then_inc(s_pc, 1)
                pool.wait_ge(s_pc, n[0])

            link(nc.gpsimd.memset(ident[:], 0.0))
            link(nc.gpsimd.affine_select(out=ident[:], in_=ident[:], compare_op=ALU.not_equal, fill=1.0,
                                         base=0, pattern=[[-1, P]], channel_multiplier=1))
            link(nc.gpsimd.memset(ones[:], 1.0 / DIM))
            link(nc.gpsimd.memset(patches[:, PATCH:A1], 2.0))
            link(nc.gpsimd.memset(mixw[:], 0.0))
            link(nc.gpsimd.memset(ones_row[:], 1.0))
            link(nc.gpsimd.memset(neg_half[:], -0.5))
            link(nc.gpsimd.memset(onehot_h[:], 0.0))
            for h in range(HEADS):
                link(nc.gpsimd.memset(onehot_h[:, h, h:h + 1], 1.0))
            link(nc.gpsimd.memset(y0[:], 1.0))
            link(nc.gpsimd.memset(mask[:], 1.0))
            for spare in (PAD_SEQ - 1, P - 1):
                link(nc.gpsimd.affine_select(out=mask[:], in_=mask[:], compare_op=ALU.not_equal, fill=0.0,
                                             base=-spare, pattern=[[0, 1]], channel_multiplier=1))
            link(nc.gpsimd.memset(y_sb[:], 0.0))
            pool.dma_start(xn_dram[TOKENS:TOKENS + P, :], y_sb[:]).then_inc(s_zrow, 16)
            pool.dma_start(out[TOKENS:TOKENS + P, :], y_sb[:]).then_inc(s_zrow, 16)
            pool.wait_ge(s_zrow, 32)
            nc.gpsimd.memset(ones1[:], 1.0).then_inc(s_const, 1)

            def load_patches(i):
                pool.dma_start(patches[:, 0:PATCH], patch_rows(i * P, P)).then_inc(s_patch, 16)

            pool.dma_start(patches[:, 0:PATCH], patch_rows(0, P)).then_inc(s_patch, 16)

            def stores(i):
                pool.wait_ge(T["t_acc"], i + 1)
                pool.dma_start(out_t[bass.ds(i, 1)].rearrange("a p d -> (a p) d"), acc[:]).then_inc(s_accst, 16)

            def store_xn(i):
                pool.wait_ge(T["t_xn"], i + 1)
                pool.dma_start(xn_t[bass.ds(i, 1)].rearrange("a p d -> (a p) d"), xn[:]).then_inc(s_xnst, 16)

            def powers(i):
                pool.wait_ge(T["t_vare"], i + 1)
                nc.gpsimd.tensor_tensor(rstd[:], varsum[:], neg_half[:], ALU.pow).then_inc(T["t_rstd"], 1)

            def powers2(i):
                pool.wait_ge(T["t_var2"], i + 1)
                nc.gpsimd.tensor_tensor(rstd2[:], var2[:], neg_half[:], ALU.pow).then_inc(T["t_rstd2"], 1)

            powers(0)
            pool.wait_ge(T["t_yps"], 1)
            pool.dma_start(patches[:, 0:PATCH], patch_rows(P, P)).then_inc(s_patch, 16)
            powers2(0)
            store_xn(0)
            with pool.Fori(0, TILES - 3) as i:
                powers(i + 1)
                pool.wait_ge(T["t_yps"], i + 2)
                pool.dma_start(patches[:, 0:PATCH],
                               bass.AP(tensor=x.tensor, offset=(i + 2) * (P * STRIDE), ap=[[STRIDE, P], [1, PATCH]])
                               ).then_inc(s_patch, 16)
                powers2(i + 1)
                store_xn(i + 1)
                stores(i)
            last = (TILES - 1) * P
            powers(TILES - 2)
            pool.wait_ge(T["t_yps"], TILES - 1)
            pool.dma_start(patches[0:P - 1, 0:PATCH], patch_rows(last, P - 1)).then_inc(s_patch, 16)
            pool.dma_start(patches[P - 1:P, 0:PATCH], patch_rows(last + P - 2, 1)).then_inc(s_patch, 16)
            powers2(TILES - 2)
            store_xn(TILES - 2)
            stores(TILES - 3)
            powers(TILES - 1)
            powers2(TILES - 1)
            store_xn(TILES - 1)
            stores(TILES - 2)
            stores(TILES - 1)

            link(nc.gpsimd.iota(iota_e[:], pattern=[[0, TILES], [1, EXPERTS]], base=0, channel_multiplier=0,
                                allow_small_or_imprecise_dtypes=True))
            link(nc.gpsimd.iota(iota_p[:], pattern=[[1, P]], base=0, channel_multiplier=0,
                                allow_small_or_imprecise_dtypes=True))
            link(nc.gpsimd.iota(iota_s[:], pattern=[[1, SLOT_TILES]], base=0, channel_multiplier=0,
                                allow_small_or_imprecise_dtypes=True))
            link(nc.gpsimd.iota(spare_row[:], pattern=[[0, 1]], base=TOKENS, channel_multiplier=1,
                                allow_small_or_imprecise_dtypes=True))
            link(nc.gpsimd.iota(tok_id[:], pattern=[[P, TILES]], base=0, channel_multiplier=1,
                                allow_small_or_imprecise_dtypes=True))
            link(nc.gpsimd.memset(tri[:], 1.0))
            link(nc.gpsimd.affine_select(out=tri[:], in_=tri[:], compare_op=ALU.is_gt, fill=0.0,
                                         base=0, pattern=[[1, P]], channel_multiplier=-1))
            pool.dma_start(bias_bc[:], ebias.rearrange("(a e) -> a e", a=1).broadcast_to([P, EXPERTS])).then_inc(s_zrow, 16)
            pool.wait_ge(s_zrow, 48)
            nc.gpsimd.memset(rconst_done[:], 0.0).then_inc(s_const, 1)
            pool.wait_ge(s_xnst, 16 * TILES)
            pool.wait_ge(s_accst, 16 * TILES)
            pool.wait_ge(r_done, 1)

            def gather(j, first=False):
                if not first:
                    pool.wait_ge(R["e_xps"], j)
                    pool.wait_ge(s_gather, 16 * j)
                    pool.wait_ge(R["e_act"], j)
                nc.gpsimd.tensor_copy(g_idx[:], slot_idx[:, bass.ds(j, 1)])
                nc.gpsimd.tensor_copy(score[:], slot_score[:, bass.ds(j, 1)]).then_inc(R["e_idx"], 1)
                pool.wait_ge(R["e_idx"], j + 1)
                pool.sem_inc(s_issue, 1)
                pool.indirect_dma_start(out=xg[:], out_offset=None, in_=xn_dram[:, :],
                                        in_offset=bass.IndirectOffsetOnAxis(ap=g_idx[:, 0:1], axis=0)
                                        ).then_inc(s_gather, 16)

            def scatter(j, first=False):
                if not first:
                    pool.wait_ge(s_scatter, 16 * j)
                nc.gpsimd.tensor_copy(s_idx[:], slot_idx[:, bass.ds(j, 1)]).then_inc(R["e_sidx"], 1)
                pool.wait_ge(R["e_sidx"], j + 1)
                pool.wait_ge(R["e_ysb"], j + 1)
                pool.sem_inc(s_issue, 1)
                pool.indirect_dma_start(out=out[:, :], out_offset=bass.IndirectOffsetOnAxis(ap=s_idx[:, 0:1], axis=0),
                                        in_=y_sb[:], in_offset=None, compute_op=ALU.add).then_inc(s_scatter, 16)

            gather(0, first=True)
            gather(1)
            gather(2)
            scatter(0, first=True)
            with pool.Fori(1, SLOT_TILES - 2) as j:
                gather(j + 2)
                scatter(j)
            scatter(SLOT_TILES - 2)
            scatter(SLOT_TILES - 1)
            pool.wait_ge(s_scatter, 16 * SLOT_TILES)

        @block.scalar
        def _(act_e):
            A = nc.scalar.activation

            for n in range(3 * HEADS * KT):
                act_e.wait_ge(s_wa, n + 1)
                A(qkvA[:, n // KT, n % KT, :], bank[n % 8][:, 0:A1], ACT.Copy).then_inc(s_wae, 1)
            for h in range(HEADS):
                act_e.wait_ge(s_gf, h + 1)
                b = 4 * (h % 2)
                A(GT[:, h, :], bank[b][:, 0:P], ACT.Copy)
                A(g_row[:, h:h + 1], bank[b][:, P:A1], ACT.Copy)
                A(g_col[:, h:h + 1], bank[b][:, 256:257], ACT.Copy)
                A(g00[0:1, h:h + 1], bank[b + 1][0:1, 0:1], ACT.Copy)
                A(F[:, h, :], bank[b + 2][:], ACT.Copy, scale=1.0 / HEADS)
                A(f128[0:1, h, :], bank[b + 3][0:1, :], ACT.Copy, scale=1.0 / HEADS).then_inc(s_gfe, 1)
            act_e.wait_ge(s_gfe, HEADS)
            A(rmask[0:1, :], f128[0:1, 0, 0:1], ACT.Copy).then_inc(s_folded, 1)

            def token_tile(i, attend, ffn):
                a, f = i + 1, i
                if attend:
                    act_e.wait_ge(T["t_pt"], a + 1)
                    A(PT[:], bank[0][:, 0:P], ACT.Copy).then_inc(T["t_ptsb"], 1)
                if ffn:
                    act_e.wait_ge(T["t_xtps"], f + 1)
                    A(xnT[:], bank[7][:].rearrange("p (k t) -> p k t", k=KT), ACT.Copy).then_inc(T["t_xtsb"], 1)
                if attend:
                    act_e.wait_ge(T["t_ups"], a + 1)
                    for h in range(HEADS):
                        ins = A(U[:, h, :], bank[1][:, h * P:(h + 1) * P], ACT.Identity, bias=g_col[:, h:h + 1])
                    ins.then_inc(T["t_usb"], 1)
                if ffn:
                    act_e.wait_ge(T["t_h1ps"], f + 1)
                    A(sig[:], bank[5][:, 0:HID], ACT.Exp, scale=-1.0).then_inc(T["t_exps"], 1)
                if attend:
                    act_e.wait_ge(T["t_nmx"], a + 1)
                    act_e.wait_ge(T["t_winv"], a)
                    for h in range(HEADS):
                        ins = A(ex[:, h, :], s2[:, h, :], ACT.Exp, bias=nmx[:, h:h + 1], scale=rscale[:, 0:1],
                                accum_out=esum[:, h:h + 1])
                    ins.then_inc(T["t_exp"], 1)
                    act_e.wait_ge(T["t_yps"], a + 1)
                    A(YT[:], bank[3][:, 0:HEADS * P].rearrange("p (h t) -> p h t", h=HEADS), ACT.Copy)
                    A(y0[0:HEADS, :], bank[1][0:HEADS, HEADS * P:(HEADS + 1) * P], ACT.Copy).then_inc(T["t_ysb"], 1)
                if ffn:
                    act_e.wait_ge(T["t_htps"], f + 1)
                    A(hT[0:HB], bank[3][0:HB, :].rearrange("p (k t) -> p k t", k=KT), ACT.Copy).then_inc(T["t_htsb"], 1)
                if attend:
                    act_e.wait_ge(T["t_xn"], a + 1)
                    act_e.wait_ge(T["t_acc"], a)
                    A(h2[:], bank[4][:], ACT.Copy).then_inc(T["t_h2sb"], 1)

            act_e.wait_ge(s_const, 1)
            token_tile(-1, True, False)
            token_tile(0, True, True)
            with act_e.Fori(1, TILES - 1) as i:
                token_tile(i, True, True)
            token_tile(TILES - 1, False, True)

            act_e.wait_ge(r_ez, 1)
            A(prob[:], z[:], ACT.Exp).then_inc(r_exp, 1)

            def x_out(j):
                act_e.wait_ge(R["e_xps"], j + 1)
                act_e.wait_ge(R["e_h3ps"], j)
                A(xgT[:], bank[0][:].rearrange("p (k t) -> p k t", k=KT), ACT.Copy).then_inc(R["e_xsb"], 1)

            def expo(j):
                act_e.wait_ge(R["e_h1ps"], j + 1)
                act_e.wait_ge(R["e_idx"], j + 1)
                act_e.wait_ge(R["e_act"], j)
                A(rgate[:], bank[1][:, 0:HID], ACT.Silu, scale=score[:, 0:1]).then_inc(R["e_gate"], 1)

            def h_out(j):
                act_e.wait_ge(R["e_htps"], j + 1)
                A(rhT[0:HB], bank[3][0:HB, :].rearrange("p (k t) -> p k t", k=KT), ACT.Copy).then_inc(R["e_htsb"], 1)

            x_out(0)
            expo(0)
            x_out(1)
            with act_e.Fori(1, SLOT_TILES - 1) as j:
                h_out(j - 1)
                expo(j)
                x_out(j + 1)
            h_out(SLOT_TILES - 2)
            expo(SLOT_TILES - 1)
            h_out(SLOT_TILES - 1)

        @block.vector
        def _(dve):
            V = nc.vector
            n = [0]

            def link(ins):
                n[0] += 1
                ins.then_inc(s_dv, 1)
                dve.wait_ge(s_dv, n[0])

            dve.wait_ge(s_tok, 32)
            dve.wait_ge(s_mean, 1)
            link(V.tensor_copy(A_mean[:], bank[0][:, 0:A1]))
            link(V.tensor_tensor(A_T[:], A_T[:], A_mean[:].unsqueeze(1).broadcast_to([P, KT, A1]), ALU.subtract))
            V.tensor_tensor(bc2[:].unsqueeze(2), A_T[:, :, PATCH:A1], A_T[:, :, PATCH:A1], ALU.mult).then_inc(s_cen, 1)
            dve.wait_ge(s_sps, 1)
            V.tensor_scalar(S[:], bank[1][:, 0:A1], 1.0 / DIM, None, ALU.mult)
            V.tensor_scalar(s00e[:], bank[2][:, 0:1], EPS, None, ALU.add).then_inc(s_ssb, 1)
            dve.wait_ge(s_ssb, 1)
            dve.wait_ge(s_const, 1)

            def token_tile(i, attend, ffn):
                a, f = i + 1, i

                def step(name, at, ins):
                    ins.then_inc(T[name], 1)
                    dve.wait_ge(T[name], at + 1)

                if attend:
                    dve.wait_ge(T["t_sps"], a + 1)
                    dve.wait_ge(T["t_cps"], a + 1)
                    V.tensor_copy(c_sb[:], bank[0][:, 384:384 + HEADS]).then_inc(T["t_csb"], 1)
                    step("t_var", a, V.tensor_tensor_reduce(out=dots[:], in0=bank[0][:, P:P + A1], in1=patches[:],
                                                            scale=1.0, scalar=0.0, op0=ALU.mult, op1=ALU.add,
                                                            accum_out=varsum[:]))
                    V.tensor_scalar(varsum[:], varsum[:], s00e[:, 0:1], None, ALU.add).then_inc(T["t_vare"], 1)
                    dve.wait_ge(T["t_rstd"], a + 1)
                    V.tensor_scalar(diag[:], ident[:], rstd[:, 0:1], None, ALU.mult).then_inc(T["t_diag"], 1)
                    V.tensor_scalar(rscale[:], rstd[:], float(DIM) ** -0.5, None, ALU.mult)
                    V.tensor_tensor(rmask[:], rstd[:], mask[:], ALU.mult).then_inc(T["t_rm"], 1)
                if ffn:
                    dve.wait_ge(T["t_gps"], f + 1)
                    V.tensor_copy(logits[:, bass.ds(f, 1), :].rearrange("p a e -> p (a e)"),
                                  bank[2][:, 256:256 + EXPERTS]).then_inc(T["t_lg"], 1)
                if attend:
                    dve.wait_ge(T["t_rps"], a + 1)
                    V.tensor_copy(Rbc[:], bank[0][:, 448:448 + PAD_SEQ]).then_inc(T["t_rbc"], 1)
                    dve.wait_ge(T["t_csb"], a + 1)
                    dve.wait_ge(T["t_scps"], a + 1)
                    step("t_s1", a, V.tensor_tensor(
                        s1[:], bank[2][:, 0:HEADS * PAD_SEQ].rearrange("p (h n) -> p h n", h=HEADS)[:, :, 0:SEQ],
                        c_sb[:].unsqueeze(2).broadcast_to([P, HEADS, SEQ]), ALU.add))
                    dve.wait_ge(T["t_rbc"], a + 1)
                    step("t_s2", a, V.tensor_tensor(
                        s2[:], s1[:], Rbc[:, 0:SEQ].unsqueeze(1).broadcast_to([P, HEADS, SEQ]), ALU.mult))
                    step("t_mx", a, V.reduce_max(mx[:], s2[:], axis=AX.X))
                    dve.wait_ge(T["t_rm"], a + 1)
                    V.tensor_scalar(nmx[:], mx[:], rscale[:, 0:1], -1.0, ALU.mult, ALU.mult).then_inc(T["t_nmx"], 1)
                if ffn:
                    dve.wait_ge(T["t_exps"], f + 1)
                    step("t_sigd", f, V.tensor_scalar(sig[:], sig[:], 1.0, None, ALU.add))
                    step("t_sig", f, V.reciprocal(sig[:], sig[:]))
                if attend:
                    dve.wait_ge(T["t_exp"], a + 1)
                    step("t_esi", a, V.reciprocal(winv[:], esum[:]))
                    step("t_winv", a, V.tensor_scalar(winv[:], winv[:], rmask[:, 0:1], None, ALU.mult))
                    for half in range(2):
                        q = slice(half * PAD_SEQ, (half + 1) * PAD_SEQ)
                        ins = V.tensor_tensor(mixw[q, :, half * PAD_SEQ:half * PAD_SEQ + SEQ], ex[q],
                                              winv[q].unsqueeze(2).broadcast_to([PAD_SEQ, HEADS, SEQ]), ALU.mult)
                    ins.then_inc(T["t_mixw"], 1)
                if ffn:
                    step("t_sact", f, V.tensor_tensor(act[:], bank[5][:, 0:HID], sig[:], ALU.mult))
                    dve.wait_ge(T["t_h3ps"], f + 1)
                    V.tensor_tensor(act[:], bank[6][:, 0:HID], act[:], ALU.mult).then_inc(T["t_act"], 1)
                if attend:
                    dve.wait_ge(T["t_h2ps"], a + 1)
                    V.bn_stats(stats[:], bank[4][:]).then_inc(T["t_stats"], 1)
                    dve.wait_ge(s_const, 1)
                    dve.wait_ge(T["t_stats"], a + 1)
                    step("t_aggr", a, V.bn_aggr(aggr[:], stats[:]))
                    V.tensor_scalar(var2[:], aggr[:, 1:2], EPS, None, ALU.add).then_inc(T["t_var2"], 1)
                    dve.wait_ge(T["t_rstd2"], a + 1)
                    dve.wait_ge(s_xnst, 16 * a)
                    V.tensor_scalar(xn[:], bank[4][:], aggr[:, 0:1], rstd2[:, 0:1], ALU.subtract,
                                    ALU.mult).then_inc(T["t_xn"], 1)
                if ffn:
                    dve.wait_ge(T["t_ops"], f + 1)
                    dve.wait_ge(T["t_h2sb"], f + 1)
                    dve.wait_ge(s_accst, 16 * f)
                    V.tensor_tensor(acc[:], bank[5][:], h2[:], ALU.add).then_inc(T["t_acc"], 1)

            token_tile(-1, True, False)
            token_tile(0, True, True)
            with dve.Fori(1, TILES - 1) as i:
                token_tile(i, True, True)
            token_tile(TILES - 1, False, True)

            dve.wait_ge(s_const, 2)

            def bc(col):
                return col.unsqueeze(2).broadcast_to([P, TILES, EXPERTS])
            bias_te = bias_bc[:].unsqueeze(1).broadcast_to([P, TILES, EXPERTS])
            dve.wait_ge(T["t_lg"], TILES)
            link(V.reduce_max(rmx[:], logits[:], axis=AX.X))
            V.tensor_tensor(z[:], logits[:], bc(rmx[:]), ALU.subtract).then_inc(r_ez, 1)
            dve.wait_ge(r_exp, 1)
            link(V.reduce_sum(rsum[:], prob[:], axis=AX.X))
            link(V.reciprocal(rsum[:], rsum[:]))
            link(V.tensor_tensor(prob[:], prob[:], bc(rsum[:]), ALU.mult))
            link(V.tensor_tensor(choice[:], prob[:], bias_te, ALU.add))

            def best(v, i, oh, k):
                link(V.reduce_max(v[:], choice[:], axis=AX.X))
                link(V.tensor_tensor(eq[:], choice[:], bc(v[:]), ALU.is_ge))
                link(V.scalar_tensor_tensor(out=eq[:], in0=eq[:], scalar=-float(EXPERTS), in1=iota_e[:],
                                            op0=ALU.mult, op1=ALU.add))
                link(V.tensor_reduce(i[:], eq[:], axis=AX.X, op=ALU.min))
                link(V.tensor_scalar(i[:], i[:], float(EXPERTS), None, ALU.add))
                link(V.tensor_tensor(oh[:], iota_e[:], bc(i[:]), ALU.is_equal))
                link(V.tensor_tensor(tmp[:], oh[:], prob[:], ALU.mult))
                link(V.reduce_sum(prob_k[:, k, :], tmp[:], axis=AX.X))

            best(v1, i1, oh1, 0)
            link(V.scalar_tensor_tensor(out=choice[:], in0=oh1[:], scalar=-3.0e38, in1=choice[:],
                                        op0=ALU.mult, op1=ALU.add))
            best(v2, i2, oh2, 1)
            V.tensor_tensor(M[:], oh1[:], oh2[:], ALU.add).then_inc(r_M, 1)
            dve.wait_ge(r_rank, 1)
            rank_ps = bank[0][:, 0:TE].rearrange("p (t e) -> p t e", t=TILES)
            link(V.tensor_scalar(tmp[:], bank[1][:, 0:TE].rearrange("p (t e) -> p t e", t=TILES), float(DIM), None,
                                 ALU.mult))
            link(V.memset(z[:], 1.0))
            for e in range(EXPERTS):
                last = V.tensor_tensor_scan(incl[:, :, e], z[:, :, e], tmp[:, :, e], 0.0, ALU.mult, ALU.add)
            link(last)
            link(V.tensor_scalar(totals[:], incl[:, TILES - 1, :], float(P - 1), None, ALU.add))
            link(V.tensor_copy(int_e[:], totals[:]))
            link(V.tensor_scalar(int_e[:], int_e[:], LOG_P, None, ALU.logical_shift_right))
            link(V.tensor_copy(ntiles[:], int_e[:]))
            link(V.tensor_tensor_scan(ends[:], z[:, 0, :], ntiles[:], 0.0, ALU.mult, ALU.add))
            link(V.tensor_tensor(starts[:], ends[:], ntiles[:], ALU.subtract))
            link(V.tensor_tensor(incl[:], incl[:], tmp[:], ALU.subtract))
            link(V.tensor_tensor(incl[:], incl[:], rank_ps, ALU.add))
            link(V.scalar_tensor_tensor(out=pos[:], in0=starts[:].unsqueeze(1).broadcast_to([P, TILES, EXPERTS]),
                                        scalar=float(P), in1=incl[:], op0=ALU.mult, op1=ALU.add))
            for k, oh in enumerate((oh1, oh2)):
                link(V.tensor_tensor(tmp[:], oh[:], pos[:], ALU.mult))
                link(V.reduce_sum(pk[:, k, :], tmp[:], axis=AX.X))
            link(V.tensor_copy(int_k[:], pk[:]))
            link(V.tensor_scalar(int_low[:], int_k[:], P - 1, None, ALU.bitwise_and))
            link(V.tensor_copy(low[:], int_low[:]))
            link(V.tensor_scalar(int_k[:], int_k[:], LOG_P, None, ALU.logical_shift_right))
            link(V.tensor_copy(hi[:], int_k[:]))
            link(V.tensor_tensor(val[:], tok_id[:].unsqueeze(1).broadcast_to([P, TOPK, TILES]), low[:], ALU.subtract))
            link(V.tensor_scalar(val[:], val[:], -float(TOKENS), None, ALU.add))
            link(V.tensor_tensor(te_cmp[:], iota_s[0:1, :].unsqueeze(2).broadcast_to([1, SLOT_TILES, EXPERTS]),
                                 ends[0:1, :].unsqueeze(1).broadcast_to([1, SLOT_TILES, EXPERTS]), ALU.is_ge))
            link(V.reduce_sum(te_sum[:], te_cmp[:], axis=AX.X))
            link(V.tensor_scalar(tile_expert[:], te_sum[:], float(EXPERTS - 1), None, ALU.min))

            lowf = low[:].rearrange("p k t -> p (k t)")
            hif, valf, probf = (v[:].rearrange("p k t -> p (k t)") for v in (hi, val, prob_k))
            def onehot_rows(g, b):
                cols = bass.ds((2 * g + b) * CG, CG)
                V.tensor_tensor(hihot[b][:], iota_s[:].unsqueeze(1).broadcast_to([P, CG, SLOT_TILES]),
                                hif[:, cols].unsqueeze(2).broadcast_to([P, CG, SLOT_TILES]),
                                ALU.is_equal).then_inc(r_oh, 1)
                V.tensor_tensor(lowhot[b][:], iota_p[:].unsqueeze(1).broadcast_to([P, CG, P]),
                                lowf[:, cols].unsqueeze(2).broadcast_to([P, CG, P]), ALU.is_equal)
                dve.wait_ge(r_oh, 4 * g + 2 * b + 1)
                V.tensor_tensor(hival[b][:, :, 0:SLOT_TILES], hihot[b][:],
                                valf[:, cols].unsqueeze(2).broadcast_to([P, CG, SLOT_TILES]), ALU.mult)
                V.tensor_tensor(hival[b][:, :, SLOT_TILES:], hihot[b][:],
                                probf[:, cols].unsqueeze(2).broadcast_to([P, CG, SLOT_TILES]),
                                ALU.mult).then_inc(r_oh, 1)

            onehot_rows(0, 0)
            onehot_rows(0, 1)
            with dve.Fori(1, C // (2 * CG)) as g:
                dve.wait_ge(r_ohused, 2 * g)
                onehot_rows(g, 0)
                onehot_rows(g, 1)
            dve.wait_ge(r_list, 1)
            V.tensor_scalar(slot_idx[:], bank[2][:, 0:SLOT_TILES], spare_row[:, 0:1], None, ALU.add)
            V.tensor_copy(slot_score[:], bank[2][:, SLOT_TILES:2 * SLOT_TILES]).then_inc(r_done, 1)

            def gate(j):
                dve.wait_ge(R["e_gate"], j + 1)
                dve.wait_ge(R["e_h3ps"], j + 1)
                dve.wait_ge(R["e_htps"], j)
                V.scalar_tensor_tensor(out=ract[:], in0=bank[2][:, 0:HID], scalar=score[:, 0:1], in1=rgate[:],
                                       op0=ALU.mult, op1=ALU.mult).then_inc(R["e_act"], 1)

            def y_out(j):
                dve.wait_ge(R["e_yps"], j + 1)
                dve.wait_ge(s_scatter, 16 * j)
                V.tensor_copy(y_sb[:], bank[4][:]).then_inc(R["e_ysb"], 1)

            gate(0)
            with dve.Fori(1, SLOT_TILES) as j:
                gate(j)
                y_out(j - 1)
            y_out(SLOT_TILES - 1)

        @block.tensor
        def _(pe):
            MM = nc.tensor.matmul

            pe.wait_ge(s_tok, 32)
            pe.wait_ge(s_const, 1)
            for k in range(KT):
                ins = MM(bank[0][:, 0:A1], ones[:], A_T[:, k, :], start=k == 0, stop=k == KT - 1)
            ins.then_inc(s_mean, 1)
            pe.wait_ge(s_cen, 1)
            for k in range(KT):
                MM(bank[1][:, 0:A1], A_T[:, k, 0:P], A_T[:, k, :], start=k == 0, stop=k == KT - 1)
            for k in range(KT):
                ins = MM(bank[2][:, 0:1], ones[:], bc2[:, k:k + 1], start=k == 0, stop=k == KT - 1)
            ins.then_inc(s_sps, 1)
            pe.wait_ge(s_ssb, 1)
            for n in range(3 * HEADS * KT):
                m, db = n // KT, n % KT
                if db == 0:
                    pe.wait_ge(s_qkv, 16 * 3 * HEADS)
                if n >= 8:
                    pe.wait_ge(s_wae, n - 7)
                for k in range(KT):
                    ins = MM(bank[n % 8][:, 0:A1], qkvT[:, m, k, db * P:(db + 1) * P], A_T[:, k, :],
                             start=k == 0, stop=k == KT - 1)
                ins.then_inc(s_wa, 1)
            pe.wait_ge(s_wae, 3 * HEADS * KT)
            pe.wait_ge(s_fc, 16)
            for h in range(HEADS):
                QA, KA, VA = qkvA[:, h], qkvA[:, HEADS + h], qkvA[:, 2 * HEADS + h]
                if h >= 2:
                    pe.wait_ge(s_gfe, h - 1)
                b = 4 * (h % 2)
                for dst, lhs, rhs in ((bank[b][:, 0:A1], KA[:, :, 0:P], QA[:, :, :]),
                                      (bank[b][:, 256:257], QA[:, :, 0:P], KA[:, :, P:A1]),
                                      (bank[b + 1][0:1, 0:1], QA[:, :, P:A1], KA[:, :, P:A1]),
                                      (bank[b + 2][:], VA[:, :, 0:P], fcT_sb[:]),
                                      (bank[b + 3][0:1, :], VA[:, :, P:A1], fcT_sb[:])):
                    for k in range(KT):
                        ins = MM(dst, lhs[:, k, :], rhs[:, k, :], start=k == 0, stop=k == KT - 1)
                ins.then_inc(s_gf, 1)
            pe.wait_ge(s_gfe, HEADS)
            pe.wait_ge(s_bload, 16 * 7)
            pe.wait_ge(s_tail, 16 * HEADS)

            def token_tile(i, attend, ffn, last_attend=False):
                a, f = i + 1, i
                if attend:
                    pe.wait_ge(s_patch, 16 * a + 16 + (16 if last_attend else 0))
                    pe.wait_ge(T["t_rbc"], a)
                    nc.tensor.transpose(bank[0][:, 0:P], patches[:, 0:P], ident[:]).then_inc(T["t_pt"], 1)
                if ffn:
                    pe.wait_ge(T["t_xn"], f + 1)
                    for k in range(KT):
                        ins = nc.tensor.transpose(bank[7][:, k * P:(k + 1) * P], xn[:, k * P:(k + 1) * P], ident[:])
                    ins.then_inc(T["t_xtps"], 1)
                if attend:
                    pe.wait_ge(T["t_ptsb"], a + 1)
                    MM(bank[0][:, P:P + A1], PT[:], S[:], start=True, stop=True).then_inc(T["t_sps"], 1)
                    MM(bank[0][:, 384:384 + HEADS], PT[:], g_row[:], start=True, stop=False)
                    MM(bank[0][:, 384:384 + HEADS], ones_row[0:1, :], g00[0:1, :], start=False, stop=True).then_inc(T["t_cps"], 1)
                    pe.wait_ge(T["t_ysb"], a)
                    for h in range(HEADS):
                        ins = MM(bank[1][:, h * P:(h + 1) * P], GT[:, h, :], PT[:], start=True, stop=True)
                    ins.then_inc(T["t_ups"], 1)
                if ffn:
                    pe.wait_ge(T["t_xtsb"], f + 1)
                    pe.wait_ge(T["t_s1"], f + 1)
                    for k in range(KT):
                        ins = MM(bank[2][:, 256:256 + EXPERTS], xnT[:, k, :], gw_sb[:, k, :], start=k == 0, stop=k == KT - 1)
                    ins.then_inc(T["t_gps"], 1)
                    pe.wait_ge(T["t_acc"], f)
                    for k in range(KT):
                        ins = MM(bank[5][:, 0:HID], xnT[:, k, :], sw1_sb[:, k, :], start=k == 0, stop=k == KT - 1)
                    ins.then_inc(T["t_h1ps"], 1)
                if attend:
                    pe.wait_ge(T["t_diag"], a + 1)
                    for half in range(2):
                        q = slice(half * PAD_SEQ, (half + 1) * PAD_SEQ)
                        ins = MM(bank[0][q, 448:448 + PAD_SEQ], ones1[:], diag[:, q], start=True, stop=True)
                    ins.then_inc(T["t_rps"], 1)
                    pe.wait_ge(T["t_usb"], a + 1)
                    if ffn:
                        pe.wait_ge(T["t_lg"], f + 1)
                    for h in range(HEADS):
                        for half in range(2):
                            q = slice(half * PAD_SEQ, (half + 1) * PAD_SEQ)
                            ins = MM(bank[2][q, h * PAD_SEQ:(h + 1) * PAD_SEQ], U[:, h, q], PT[:, q],
                                     start=True, stop=True)
                    ins.then_inc(T["t_scps"], 1)
                if ffn:
                    for k in range(KT):
                        ins = MM(bank[6][:, 0:HID], xnT[:, k, :], sw3_sb[:, k, :], start=k == 0, stop=k == KT - 1)
                    ins.then_inc(T["t_h3ps"], 1)
                if attend:
                    pe.wait_ge(T["t_h2sb"], a)
                    MM(bank[4][:], PT[:], tokWT_sb[:], start=True, stop=False)
                    pe.wait_ge(T["t_mixw"], a + 1)
                    MM(bank[3][:, 0:HEADS * P], patches[:, 0:P], mixw[:].rearrange("p h t -> p (h t)"),
                       start=True, stop=True)
                    for h in range(HEADS):
                        ins = MM(bank[1][0:HEADS, HEADS * P:(HEADS + 1) * P], onehot_h[:, h, :], mixw[:, h, :],
                                 start=h == 0, stop=h == HEADS - 1)
                    ins.then_inc(T["t_yps"], 1)
                if ffn:
                    pe.wait_ge(T["t_act"], f + 1)
                    if attend:
                        pe.wait_ge(T["t_ysb"], a + 1)
                    for k in range(KT):
                        ins = nc.tensor.transpose(bank[3][0:HB, k * P:(k + 1) * P], act[:, k * HB:(k + 1) * HB], ident[:])
                    ins.then_inc(T["t_htps"], 1)
                if attend:
                    pe.wait_ge(T["t_ysb"], a + 1)
                    for h in range(HEADS):
                        MM(bank[4][:], YT[:, h, :], F[:, h, :], start=False, stop=False)
                    MM(bank[4][:], y0[0:HEADS + 2, :], tail[:], start=False, stop=True).then_inc(T["t_h2ps"], 1)
                if ffn:
                    pe.wait_ge(T["t_htsb"], f + 1)
                    for k in range(KT):
                        ins = MM(bank[5][:], hT[0:HB, k, :], sw2_sb[:, k, :], start=k == 0, stop=k == KT - 1)
                    ins.then_inc(T["t_ops"], 1)

            token_tile(-1, True, False)
            token_tile(0, True, True)
            with pe.Fori(1, TILES - 2) as i:
                token_tile(i, True, True)
            token_tile(TILES - 2, True, True, last_attend=True)
            token_tile(TILES - 1, False, True)

            pe.wait_ge(r_M, 1)
            Mf = M[:].rearrange("p t e -> p (t e)")
            MM(bank[0][:, 0:TE], tri[:], Mf, start=True, stop=True)
            MM(bank[1][:, 0:TE], ones[:], Mf, start=True, stop=True).then_inc(r_rank, 1)

            def list_group(g, b, first, last):
                pe.wait_ge(r_oh, 4 * g + 2 * b + 2)
                for c in range(CG):
                    ins = MM(bank[2][:, 0:2 * SLOT_TILES], lowhot[b][:, c, :], hival[b][:, c, :],
                             start=first and c == 0, stop=last and c == CG - 1)
                ins.then_inc(r_ohused, 1)
                return ins

            G = C // (2 * CG)
            list_group(0, 0, True, False)
            list_group(0, 1, False, False)
            with pe.Fori(1, G - 1) as g:
                list_group(g, 0, False, False)
                list_group(g, 1, False, False)
            list_group(G - 1, 0, False, False)
            list_group(G - 1, 1, False, True)
            nc.tensor.transpose(bank[3][:, 0:P], ident[:], ident[:]).then_inc(r_list, 1)
            pe.wait_ge(r_done, 1)

            def transpose_rows(j):
                pe.wait_ge(s_gather, 16 * j + 16)
                pe.wait_ge(R["e_xsb"], j)
                for k in range(KT):
                    ins = nc.tensor.transpose(bank[0][:, k * P:(k + 1) * P], xg[:, k * P:(k + 1) * P], ident[:])
                ins.then_inc(R["e_xps"], 1)

            def up(j, e, third, dst, done):
                for k in range(KT):
                    o = e * W_WORDS + (third * KT + k) * HID
                    ins = MM(dst[:, 0:HID], xgT[:, k, :], experts[:, bass.ds(o, HID)], start=k == 0, stop=k == KT - 1)
                ins.then_inc(done, 1)

            def transpose_hidden(j):
                pe.wait_ge(R["e_act"], j + 1)
                for k in range(KT):
                    ins = nc.tensor.transpose(bank[3][0:HB, k * P:(k + 1) * P], ract[:, k * HB:(k + 1) * HB], ident[:])
                ins.then_inc(R["e_htps"], 1)

            def down(j, e):
                pe.wait_ge(R["e_htsb"], j + 1)
                pe.wait_ge(R["e_ysb"], j)
                for k in range(KT):
                    o = e * W_WORDS + 2 * KT * HID + k * DIM
                    ins = MM(bank[4][:], rhT[0:HB, k, :], experts[0:HB, bass.ds(o, DIM)], start=k == 0, stop=k == KT - 1)
                ins.then_inc(R["e_yps"], 1)

            def expert_of(j):
                return pe.value_load(tile_expert[0:1, bass.ds(j, 1)], min_val=0, max_val=EXPERTS - 1)

            def slot_tile(j, before, after):
                e = expert_of(j)
                pe.wait_ge(s_expert, 48 * e + 48)
                pe.wait_ge(R["e_xsb"], j + 1)
                if before:
                    pe.wait_ge(R["e_act"], j)
                up(j, e, 0, bank[1], R["e_h1ps"])
                if before:
                    transpose_hidden(j - 1)
                up(j, e, 1, bank[2], R["e_h3ps"])
                if after:
                    transpose_rows(j + 1)
                if before:
                    down(j - 1, expert_of(j - 1))

            transpose_rows(0)
            slot_tile(0, False, True)
            with pe.Fori(1, SLOT_TILES - 1) as j:
                slot_tile(j, True, True)
            slot_tile(SLOT_TILES - 1, True, False)
            transpose_hidden(SLOT_TILES - 1)
            down(SLOT_TILES - 1, expert_of(SLOT_TILES - 1))


def kernel(x, L0_tok_W, L0_tok_b, L0_attn_Wq, L0_attn_Wk, L0_attn_Wv, L0_attn_fc_w, L0_attn_fc_b, L0_ffn_gate_w,
           L0_ffn_w1, L0_ffn_w2, L0_ffn_w3, L0_ffn_sw1, L0_ffn_sw2, L0_ffn_sw3, L0_ffn_expert_bias):
    import numpy as np
    import concourse.bacc as bacc
    from concourse.bass_utils import run_bass_kernel_spmd

    def t(a):
        return np.ascontiguousarray(np.swapaxes(np.asarray(a), -1, -2))

    arrays = {
        "x": np.ascontiguousarray(np.asarray(x).reshape(-1)),
        "tokWT": t(L0_tok_W), "tokW": np.asarray(L0_tok_W), "tokb": np.asarray(L0_tok_b),
        "WqT": t(L0_attn_Wq), "WkT": t(L0_attn_Wk), "WvT": t(L0_attn_Wv), "fcT": t(L0_attn_fc_w),
        "fcb": np.asarray(L0_attn_fc_b), "gate_w": np.asarray(L0_ffn_gate_w),
        "w1": np.asarray(L0_ffn_w1), "w2": np.asarray(L0_ffn_w2), "w3": np.asarray(L0_ffn_w3),
        "sw1": np.asarray(L0_ffn_sw1), "sw2": np.asarray(L0_ffn_sw2), "sw3": np.asarray(L0_ffn_sw3),
        "ebias": np.asarray(L0_ffn_expert_bias),
    }
    nc = bacc.Bacc("TRN2", target_bir_lowering=False, num_devices=1)
    args = [nc.dram_tensor(f"in_{n}", a.shape, mybir.dt.from_np(a.dtype), kind="ExternalInput").ap()
            for n, a in arrays.items()]
    out = nc.dram_tensor("rows_out", (TOKENS + P, DIM), mybir.dt.float32, kind="ExternalOutput").ap()
    audio_tower(nc, *args, out)
    r = run_bass_kernel_spmd(nc, [{f"in_{n}": a for n, a in arrays.items()}], core_ids=[0])
    rows = r.results[0]["rows_out"]
    return rows[:TOKENS].reshape(BATCH, PAD_SEQ, DIM)[:, :SEQ]
```

```python
import concourse.bass as bass
from concourse import mybir
from contextlib import ExitStack

BATCH, SAMPLES = 64, 4096
PATCH, STRIDE = 128, 64
SEQ = (SAMPLES - PATCH) // STRIDE + 1
PAD_SEQ = 64
DIM, HEADS, HID, EXPERTS, TOPK = 512, 3, 448, 8, 2
P, LOG_P = 128, 7
TOKENS = BATCH * PAD_SEQ
TILES = TOKENS // P
KT = DIM // P
HB = HID // KT
SLOT_TILES = (TOKENS * TOPK + EXPERTS * (P - 1)) // P
assert SLOT_TILES % 2 == 1
EPS = 1e-5
A1 = PATCH + 1
W_WORDS = 2 * KT * HID + KT * DIM


def audio_tower(nc, x, tokWT, tokW, tokb, WqT, WkT, WvT, fcT, fcb, gate_w, w1, w2, w3, sw1, sw2, sw3, ebias, out):
    f32, u32 = mybir.dt.float32, mybir.dt.uint32
    ALU, ACT, AX = mybir.AluOpType, mybir.ActivationFunctionType, mybir.AxisListType
    ctx = ExitStack()
    with ctx:
        def sb(name, shape, dt=f32):
            return ctx.enter_context(nc.sbuf_tensor(name, shape, dt))

        def sem(name):
            return ctx.enter_context(nc.semaphore(name))

        xn_dram = nc.dram_tensor("xn_rows", [TOKENS + P, DIM], f32, kind="Internal").ap()

        experts = sb("experts", [P, EXPERTS * W_WORDS])
        place = [0]

        def words(n, *dims, parts=P):
            a = place[0]
            place[0] += n
            assert place[0] <= EXPERTS * W_WORDS
            v = experts[0:parts, a:a + n]
            if len(dims) == 2:
                v = v.rearrange("p (a b) -> p a b", a=dims[0])
            if len(dims) == 3:
                v = v.rearrange("p (a b c) -> p a b c", a=dims[0], b=dims[1])
            return v

        qkvT = words(3 * HEADS * KT * DIM, 3 * HEADS, KT, DIM)
        fcT_sb = words(KT * DIM, KT, DIM)
        qkvA = words(3 * HEADS * KT * A1, 3 * HEADS, KT, A1)
        A_T = words(KT * A1, KT, A1)
        EARLY = 5
        assert place[0] <= EARLY * W_WORDS - 2 * A1
        A_mean = words(A1)
        bc2 = words(KT)

        place[0] = EARLY * W_WORDS
        sw_sb = words(W_WORDS)
        sw1_sb = sw_sb[:, 0:KT * HID].rearrange("p (k h) -> p k h", k=KT)
        sw3_sb = sw_sb[:, KT * HID:2 * KT * HID].rearrange("p (k h) -> p k h", k=KT)
        sw2_sb = sw_sb[0:HB, 2 * KT * HID:].rearrange("p (k d) -> p k d", k=KT)
        F = words(HEADS * DIM, HEADS, DIM)
        tokWT_sb = words(DIM)
        tail = words(DIM, parts=HEADS + 2)
        GT = words(HEADS * P, HEADS, P)
        g_row = words(HEADS)
        g_col = words(HEADS)
        g00 = words(HEADS, parts=1)
        S = words(A1)
        s00e = words(1)
        gw_sb = words(KT * EXPERTS, KT, EXPERTS)
        patches = words(A1)
        dots = words(A1)
        PT = words(P)
        U = words(HEADS * P, HEADS, P)
        varsum, rstd, rscale, rmask = words(1), words(1), words(1), words(1)
        diag = words(P)
        c_sb = words(HEADS)
        Rbc = words(PAD_SEQ)
        s1 = words(HEADS * SEQ, HEADS, SEQ)
        s2 = words(HEADS * SEQ, HEADS, SEQ)
        mx, nmx, esum, winv = words(HEADS), words(HEADS), words(HEADS), words(HEADS)
        ex = words(HEADS * SEQ, HEADS, SEQ)
        mixw = words(HEADS * P, HEADS, P)
        YT = words(HEADS * P, HEADS, P)
        y0 = words(P, parts=HEADS + 2)
        h2 = words(DIM)
        stats, aggr, var2, rstd2 = words(6), words(2), words(1), words(1)
        neg_half = words(1)
        xn = words(DIM)
        xnT = words(DIM, KT, P)
        gate_t = words(HID)
        act = words(HID)
        hT = words(KT * P, KT, P)
        acc = words(DIM)
        onehot_h = words(HEADS * HEADS, HEADS, HEADS)
        mask = words(1)
        ones1 = words(PAD_SEQ)
        ones_row = words(P, parts=1)

        ident = sb("ident", [P, P])
        ones = sb("ones", [P, P])
        logits = sb("logits", [P, TILES, EXPERTS])
        slot_idx = sb("slot_idx", [P, SLOT_TILES], u32)
        slot_score = sb("slot_score", [P, SLOT_TILES])
        tile_expert = sb("tile_expert", [1, SLOT_TILES], u32)

        g_idx = [sb(f"g_idx{c}", [P, 1], u32) for c in range(2)]
        s_idx = sb("s_idx", [P, 1], u32)
        score = [sb(f"score{c}", [P, 1]) for c in range(2)]
        xg = [sb(f"xg{c}", [P, DIM]) for c in range(2)]
        xgT = sb("xgT", [P, KT, P])
        rgate = sb("rgate", [P, HID])
        ract = sb("ract", [P, HID])
        rhT = sb("rhT", [P, KT, P])
        y_sb = sb("y_sb", [P, DIM])

        place[0] = EARLY * W_WORDS
        TE = TILES * EXPERTS

        def te():
            return words(TE, TILES, EXPERTS)
        z, prob, choice, iota_e, eq, oh1, oh2, M, incl, pos = (te() for _ in range(10))
        tmp = te()
        rmx, rsum, v1, i1, v2, i2 = (words(TILES) for _ in range(6))
        C = TOPK * TILES
        pk, low, hi, val, prob_k = (words(C, TOPK, TILES) for _ in range(5))
        bias_bc = words(EXPERTS)
        rconst_done = words(1)
        totals, ntiles, ends, starts = (words(EXPERTS) for _ in range(4))
        int_e = words(EXPERTS).bitcast(u32)
        int_k, int_low = (words(C).bitcast(u32).rearrange("p (a b) -> p a b", a=TOPK) for _ in range(2))
        tri = words(P)
        iota_p = words(P)
        iota_s = words(SLOT_TILES)
        spare_row = words(1)
        tok_id = words(TILES)
        CG = 4
        lowhot = [words(CG * P, CG, P) for _ in range(2)]
        hihot = [words(CG * SLOT_TILES, CG, SLOT_TILES) for _ in range(2)]
        hival = [words(CG * 2 * SLOT_TILES, CG, 2 * SLOT_TILES) for _ in range(2)]
        te_cmp = words(SLOT_TILES * EXPERTS, SLOT_TILES, EXPERTS, parts=1)
        te_sum = words(SLOT_TILES, parts=1)

        bank = [ctx.enter_context(nc.psum_tensor(f"bank{i}", [P, DIM], f32)) for i in range(8)]

        s_tok, s_fc = sem("s_tok"), sem("s_fc")
        s_qkv = [sem(f"s_qkv{m}") for m in range(3 * HEADS)]
        s_bload, s_patch, s_plast = sem("s_bload"), sem("s_patch"), sem("s_plast")
        s_expert = sem("s_expert")
        s_zrow, s_xnst, s_accst = sem("s_zrow"), sem("s_xnst"), sem("s_accst")
        s_gather, s_scatter = [sem(f"s_gather{c}") for c in range(2)], sem("s_scatter")
        s_issue = sem("s_issue")
        s_const = sem("s_const")
        s_pc = sem("s_pc")
        s_dv = sem("s_dv")
        s_mean, s_cen, s_sps = sem("s_mean"), sem("s_cen"), sem("s_sps")
        s_bc2, s_ssb, s_wa, s_wae, s_gf, s_gfe = (sem(n) for n in ("s_bc2", "s_ssb", "s_wa", "s_wae", "s_gf", "s_gfe"))
        s_f128, s_folded = sem("s_f128"), sem("s_folded")
        names = ("t_vare t_var2 t_tanh t_pt t_ptsb t_sps t_cps t_ups t_var t_rstd t_diag t_usb t_csb t_rps t_rbc t_scps t_s1 t_s2 t_mx t_nmx "
                 "t_exp t_rm t_esi t_winv t_mixw t_yps t_ysb t_h2ps t_stats t_aggr t_rstd2 t_xn t_h2sb t_xtps t_xtsb "
                 "t_gps t_lg t_h1ps t_h3ps t_sact t_act t_htps t_htsb t_ops t_acc").split()
        T = {n: sem(n) for n in names}
        r_exp, r_ez, r_M, r_rank, r_oh, r_ohused, r_list, r_done = (
            sem(n) for n in ("r_exp", "r_ez", "r_M", "r_rank", "r_oh", "r_ohused", "r_list", "r_done"))
        names = "e_idx e_sidx e_xps e_xsb e_h1ps e_h3ps e_gate e_act e_htps e_htsb e_yps e_ysb".split()
        R = {n: sem(n) for n in names}

        block = ctx.enter_context(nc.Block())

        w1_d = w1.rearrange("e (k p) h -> e p k h", p=P)
        w3_d = w3.rearrange("e (k p) h -> e p k h", p=P)
        w2_d = w2.rearrange("e (k p) d -> e p k d", p=HB)
        out_t = out[0:TOKENS, :].rearrange("(t p) d -> t p d", p=P)
        xn_t = xn_dram[0:TOKENS, :].rearrange("(t p) d -> t p d", p=P)

        def expert_view(e):
            o = e * W_WORDS
            return (experts[:, o:o + KT * HID].rearrange("p (k h) -> p k h", k=KT),
                    experts[:, o + KT * HID:o + 2 * KT * HID].rearrange("p (k h) -> p k h", k=KT),
                    experts[0:HB, o + 2 * KT * HID:o + W_WORDS].rearrange("p (k d) -> p k d", k=KT))

        def patch_rows(row, n):
            return bass.AP(tensor=x.tensor, offset=row * STRIDE, ap=[[STRIDE, n], [1, PATCH]])

        @block.sync
        def _(sp):
            sp.dma_start(A_T[:, :, 0:PATCH], tokW.rearrange("(k p) q -> p k q", p=P)).then_inc(s_tok, 16)
            with nc.allow_non_contiguous_dma(reason="512 words of bias, one in a channel's partition"):
                sp.dma_start(A_T[:, :, PATCH:A1], tokb.rearrange("(k p a) -> p k a", p=P, a=1)).then_inc(s_tok, 16)
            for m, w in enumerate((WqT, WkT, WvT)):
                for h in range(HEADS):
                    sp.dma_start(qkvT[:, m * HEADS + h], w[h].rearrange("(k p) d -> p k d", p=P)).then_inc(
                        s_qkv[m * HEADS + h], 16)
            sp.dma_start(fcT_sb[:], fcT.rearrange("(k p) o -> p k o", p=P)).then_inc(s_fc, 16)
            sp.dma_start(tokWT_sb[:], tokWT[:, :]).then_inc(s_bload, 16)
            sp.dma_start(tail[HEADS:HEADS + 1, :], tokb.rearrange("(a d) -> a d", a=1)).then_inc(s_bload, 16)
            sp.dma_start(tail[HEADS + 1:HEADS + 2, :], fcb.rearrange("(a d) -> a d", a=1)).then_inc(s_bload, 16)
            sp.dma_start(gw_sb[:], gate_w.rearrange("(k p) e -> p k e", p=P)).then_inc(s_bload, 16)
            sp.dma_start(sw1_sb, sw1.rearrange("(k p) h -> p k h", p=P)).then_inc(s_bload, 16)
            sp.dma_start(sw3_sb, sw3.rearrange("(k p) h -> p k h", p=P)).then_inc(s_bload, 16)
            sp.dma_start(sw2_sb, sw2.rearrange("(k p) d -> p k d", p=HB)).then_inc(s_bload, 16)
            sp.wait_ge(s_folded, 1)
            for e in range(EARLY):
                for dst, src in zip(expert_view(e), (w1_d[e], w3_d[e], w2_d[e])):
                    sp.dma_start(dst, src).then_inc(s_expert, 16)
                sp.wait_ge(s_expert, 48 * (e + 1))
            sp.wait_ge(r_done, 1)
            for e in range(EARLY, EXPERTS):
                for dst, src in zip(expert_view(e), (w1_d[e], w3_d[e], w2_d[e])):
                    sp.dma_start(dst, src).then_inc(s_expert, 16)
                sp.wait_ge(s_expert, 48 * (e + 1))

        @block.gpsimd
        def _(pool):
            n = [0]

            def link(ins):
                n[0] += 1
                ins.then_inc(s_pc, 1)
                pool.wait_ge(s_pc, n[0])

            link(nc.gpsimd.memset(ident[:], 0.0))
            link(nc.gpsimd.affine_select(out=ident[:], in_=ident[:], compare_op=ALU.not_equal, fill=1.0,
                                         base=0, pattern=[[-1, P]], channel_multiplier=1))
            link(nc.gpsimd.memset(ones[:], 1.0 / DIM))
            link(nc.gpsimd.memset(patches[:, PATCH:A1], 2.0))
            link(nc.gpsimd.memset(mixw[:], 0.0))
            link(nc.gpsimd.memset(ones_row[:], 1.0))
            link(nc.gpsimd.memset(neg_half[:], -0.5))
            link(nc.gpsimd.memset(onehot_h[:], 0.0))
            for h in range(HEADS):
                link(nc.gpsimd.memset(onehot_h[:, h, h:h + 1], 1.0))
            link(nc.gpsimd.memset(y0[:], 1.0))
            link(nc.gpsimd.memset(mask[:], 1.0))
            for spare in (PAD_SEQ - 1, P - 1):
                link(nc.gpsimd.affine_select(out=mask[:], in_=mask[:], compare_op=ALU.not_equal, fill=0.0,
                                             base=-spare, pattern=[[0, 1]], channel_multiplier=1))
            link(nc.gpsimd.memset(y_sb[:], 0.0))
            pool.dma_start(xn_dram[TOKENS:TOKENS + P, :], y_sb[:]).then_inc(s_zrow, 16)
            pool.dma_start(out[TOKENS:TOKENS + P, :], y_sb[:]).then_inc(s_zrow, 16)
            pool.wait_ge(s_zrow, 32)
            nc.gpsimd.memset(ones1[:], 1.0).then_inc(s_const, 1)

            def load_patches(i):
                pool.dma_start(patches[:, 0:PATCH], patch_rows(i * P, P)).then_inc(s_patch, 16)

            pool.dma_start(patches[:, 0:PATCH], patch_rows(0, P)).then_inc(s_patch, 16)

            def stores(i):
                pool.wait_ge(T["t_acc"], i + 1)
                pool.dma_start(out_t[bass.ds(i, 1)].rearrange("a p d -> (a p) d"), acc[:]).then_inc(s_accst, 16)

            def store_xn(i):
                pool.wait_ge(T["t_xn"], i + 1)
                pool.dma_start(xn_t[bass.ds(i, 1)].rearrange("a p d -> (a p) d"), xn[:]).then_inc(s_xnst, 16)

            def powers(i):
                pool.wait_ge(T["t_vare"], i + 1)
                nc.gpsimd.tensor_tensor(rstd[:], varsum[:], neg_half[:], ALU.pow).then_inc(T["t_rstd"], 1)

            def powers2(i):
                pool.wait_ge(T["t_var2"], i + 1)
                nc.gpsimd.tensor_tensor(rstd2[:], var2[:], neg_half[:], ALU.pow).then_inc(T["t_rstd2"], 1)

            powers(0)
            pool.wait_ge(T["t_yps"], 1)
            pool.dma_start(patches[:, 0:PATCH], patch_rows(P, P)).then_inc(s_patch, 16)
            powers2(0)
            store_xn(0)
            with pool.Fori(0, TILES - 3) as i:
                powers(i + 1)
                pool.wait_ge(T["t_yps"], i + 2)
                pool.dma_start(patches[:, 0:PATCH],
                               bass.AP(tensor=x.tensor, offset=(i + 2) * (P * STRIDE), ap=[[STRIDE, P], [1, PATCH]])
                               ).then_inc(s_patch, 16)
                powers2(i + 1)
                store_xn(i + 1)
                stores(i)
            last = (TILES - 1) * P
            powers(TILES - 2)
            pool.wait_ge(T["t_yps"], TILES - 1)
            pool.dma_start(patches[0:P - 1, 0:PATCH], patch_rows(last, P - 1)).then_inc(s_plast, 16)
            pool.wait_ge(s_plast, 16)
            pool.dma_start(patches[P - 1:P, 0:PATCH], patch_rows(last + P - 2, 1)).then_inc(s_patch, 16)
            powers2(TILES - 2)
            store_xn(TILES - 2)
            stores(TILES - 3)
            powers(TILES - 1)
            powers2(TILES - 1)
            store_xn(TILES - 1)
            stores(TILES - 2)
            stores(TILES - 1)

            link(nc.gpsimd.iota(iota_e[:], pattern=[[0, TILES], [1, EXPERTS]], base=0, channel_multiplier=0,
                                allow_small_or_imprecise_dtypes=True))
            link(nc.gpsimd.iota(iota_p[:], pattern=[[1, P]], base=0, channel_multiplier=0,
                                allow_small_or_imprecise_dtypes=True))
            link(nc.gpsimd.iota(iota_s[:], pattern=[[1, SLOT_TILES]], base=0, channel_multiplier=0,
                                allow_small_or_imprecise_dtypes=True))
            link(nc.gpsimd.iota(spare_row[:], pattern=[[0, 1]], base=TOKENS, channel_multiplier=1,
                                allow_small_or_imprecise_dtypes=True))
            link(nc.gpsimd.iota(tok_id[:], pattern=[[P, TILES]], base=0, channel_multiplier=1,
                                allow_small_or_imprecise_dtypes=True))
            link(nc.gpsimd.memset(tri[:], 1.0))
            link(nc.gpsimd.affine_select(out=tri[:], in_=tri[:], compare_op=ALU.is_gt, fill=0.0,
                                         base=0, pattern=[[1, P]], channel_multiplier=-1))
            pool.dma_start(bias_bc[:], ebias.rearrange("(a e) -> a e", a=1).broadcast_to([P, EXPERTS])).then_inc(s_zrow, 16)
            pool.wait_ge(s_zrow, 48)
            nc.gpsimd.memset(rconst_done[:], 0.0).then_inc(s_const, 1)
            pool.wait_ge(s_xnst, 16 * TILES)
            pool.wait_ge(s_accst, 16 * TILES)
            pool.wait_ge(r_done, 1)

            def gather(t, c, first=False):
                j = 2 * t + c
                if not first:
                    pool.wait_ge(R["e_act"], j - 1)
                nc.gpsimd.tensor_copy(g_idx[c][:], slot_idx[:, bass.ds(j, 1)])
                nc.gpsimd.tensor_copy(score[c][:], slot_score[:, bass.ds(j, 1)]).then_inc(R["e_idx"], 1)
                pool.wait_ge(R["e_idx"], j + 1)
                pool.sem_inc(s_issue, 1)
                pool.indirect_dma_start(out=xg[c][:], out_offset=None, in_=xn_dram[:, :],
                                        in_offset=bass.IndirectOffsetOnAxis(ap=g_idx[c][:, 0:1], axis=0)
                                        ).then_inc(s_gather[c], 16)

            def scatter(j, first=False):
                if not first:
                    pool.wait_ge(s_scatter, 16 * j)
                nc.gpsimd.tensor_copy(s_idx[:], slot_idx[:, bass.ds(j, 1)]).then_inc(R["e_sidx"], 1)
                pool.wait_ge(R["e_sidx"], j + 1)
                pool.wait_ge(R["e_ysb"], j + 1)
                pool.sem_inc(s_issue, 1)
                pool.indirect_dma_start(out=out[:, :], out_offset=bass.IndirectOffsetOnAxis(ap=s_idx[:, 0:1], axis=0),
                                        in_=y_sb[:], in_offset=None, compute_op=ALU.add).then_inc(s_scatter, 16)

            gather(0, 0, first=True)
            gather(0, 1, first=True)
            gather(1, 0)
            scatter(0, first=True)
            gather(1, 1)
            scatter(1)
            with pool.Fori(2, SLOT_TILES // 2) as t:
                gather(t, 0)
                scatter(2 * t - 2)
                gather(t, 1)
                scatter(2 * t - 1)
            gather(SLOT_TILES // 2, 0)
            for j in range(SLOT_TILES - 3, SLOT_TILES):
                scatter(j)
            pool.wait_ge(s_scatter, 16 * SLOT_TILES)

        @block.scalar
        def _(act_e):
            A = nc.scalar.activation

            for n in range(3 * HEADS * KT):
                act_e.wait_ge(s_wa, n + 1)
                A(qkvA[:, n // KT, n % KT, :], bank[n % 8][:, 0:A1], ACT.Copy).then_inc(s_wae, 1)
            for h in range(HEADS):
                act_e.wait_ge(s_gf, h + 1)
                b = 4 * (h % 2)
                A(GT[:, h, :], bank[b][:, 0:P], ACT.Copy)
                A(g_row[:, h:h + 1], bank[b][:, P:A1], ACT.Copy)
                A(g_col[:, h:h + 1], bank[b][:, 256:257], ACT.Copy)
                A(g00[0:1, h:h + 1], bank[b + 1][0:1, 0:1], ACT.Copy)
                A(F[:, h, :], bank[b + 2][:], ACT.Copy, scale=1.0 / HEADS).then_inc(s_gfe, 1)
            act_e.wait_ge(s_f128, 1)
            A(tail[0:HEADS, :], bank[3][0:HEADS, :], ACT.Copy, scale=1.0 / HEADS).then_inc(s_folded, 1)

            def patches_out(a):
                act_e.wait_ge(T["t_pt"], a + 1)
                A(PT[:], bank[0][:, 0:P], ACT.Copy).then_inc(T["t_ptsb"], 1)

            def token_tile(i, attend, ffn, more=True):
                a, f = i + 1, i
                if ffn:
                    act_e.wait_ge(T["t_xtps"], f + 1)
                    A(xnT[:], bank[7][:].rearrange("p (k t) -> p k t", k=KT), ACT.Copy).then_inc(T["t_xtsb"], 1)
                if attend:
                    act_e.wait_ge(T["t_ups"], a + 1)
                    for h in range(HEADS):
                        ins = A(U[:, h, :], bank[1][:, h * P:(h + 1) * P], ACT.Identity, bias=g_col[:, h:h + 1])
                    ins.then_inc(T["t_usb"], 1)
                if ffn:
                    act_e.wait_ge(T["t_h1ps"], f + 1)
                    A(gate_t[:], bank[5][:, 0:HID], ACT.Tanh, scale=0.5).then_inc(T["t_tanh"], 1)
                if attend:
                    act_e.wait_ge(T["t_nmx"], a + 1)
                    for h in range(HEADS):
                        ins = A(ex[:, h, :], s2[:, h, :], ACT.Exp, bias=nmx[:, h:h + 1], scale=rscale[:, 0:1],
                                accum_out=esum[:, h:h + 1])
                    ins.then_inc(T["t_exp"], 1)
                    act_e.wait_ge(T["t_yps"], a + 1)
                    A(YT[:], bank[3][:, 0:HEADS * P].rearrange("p (h t) -> p h t", h=HEADS), ACT.Copy)
                    A(y0[0:HEADS, :], bank[1][0:HEADS, HEADS * P:(HEADS + 1) * P], ACT.Copy).then_inc(T["t_ysb"], 1)
                if ffn:
                    act_e.wait_ge(T["t_htps"], f + 1)
                    A(hT[0:HB], bank[3][0:HB, :].rearrange("p (k t) -> p k t", k=KT), ACT.Copy).then_inc(T["t_htsb"], 1)
                if attend:
                    if more:
                        patches_out(a + 1)
                    act_e.wait_ge(T["t_xn"], a + 1)
                    if ffn:
                        act_e.wait_ge(T["t_acc"], a)
                    A(h2[:], bank[4][:], ACT.Copy).then_inc(T["t_h2sb"], 1)

            act_e.wait_ge(s_const, 1)
            patches_out(0)
            token_tile(-1, True, False)
            token_tile(0, True, True)
            with act_e.Fori(1, TILES - 2) as i:
                token_tile(i, True, True)
            token_tile(TILES - 2, True, True, more=False)
            token_tile(TILES - 1, False, True)

            act_e.wait_ge(r_ez, 1)
            A(prob[:], z[:], ACT.Exp).then_inc(r_exp, 1)

            def x_out(j):
                act_e.wait_ge(R["e_xps"], j + 1)
                act_e.wait_ge(R["e_h3ps"], j)
                A(xgT[:], bank[0][:].rearrange("p (k t) -> p k t", k=KT), ACT.Copy).then_inc(R["e_xsb"], 1)

            def silu(t, c):
                j = 2 * t + c
                act_e.wait_ge(R["e_h1ps"], j + 1)
                act_e.wait_ge(R["e_idx"], j + 1)
                act_e.wait_ge(R["e_act"], j)
                A(rgate[:], bank[1][:, 0:HID], ACT.Silu, scale=score[c][:, 0:1]).then_inc(R["e_gate"], 1)

            def h_out(j):
                act_e.wait_ge(R["e_htps"], j + 1)
                A(rhT[0:HB], bank[3][0:HB, :].rearrange("p (k t) -> p k t", k=KT), ACT.Copy).then_inc(R["e_htsb"], 1)

            x_out(0)
            silu(0, 0)
            x_out(1)
            h_out(0)
            silu(0, 1)
            x_out(2)
            with act_e.Fori(1, SLOT_TILES // 2) as t:
                for c in range(2):
                    h_out(2 * t + c - 1)
                    silu(t, c)
                    x_out(2 * t + c + 1)
            h_out(SLOT_TILES - 2)
            silu(SLOT_TILES // 2, 0)
            h_out(SLOT_TILES - 1)

        @block.vector
        def _(dve):
            V = nc.vector
            n = [0]

            def link(ins):
                n[0] += 1
                ins.then_inc(s_dv, 1)
                dve.wait_ge(s_dv, n[0])

            dve.wait_ge(s_tok, 32)
            dve.wait_ge(s_mean, 1)
            link(V.tensor_copy(A_mean[:], bank[0][:, 0:A1]))
            link(V.tensor_tensor(A_T[:], A_T[:], A_mean[:].unsqueeze(1).broadcast_to([P, KT, A1]), ALU.subtract))
            V.tensor_tensor(bc2[:].unsqueeze(2), A_T[:, :, PATCH:A1], A_T[:, :, PATCH:A1], ALU.mult).then_inc(s_cen, 1)
            dve.wait_ge(s_sps, 1)
            V.tensor_scalar(S[:], bank[1][:, 0:A1], 1.0 / DIM, None, ALU.mult)
            V.tensor_scalar(s00e[:], bank[2][:, 0:1], EPS, None, ALU.add).then_inc(s_ssb, 1)
            dve.wait_ge(s_ssb, 1)
            dve.wait_ge(s_const, 1)

            def token_tile(i, attend, ffn):
                a, f = i + 1, i

                def step(name, at, ins):
                    ins.then_inc(T[name], 1)
                    dve.wait_ge(T[name], at + 1)

                if attend:
                    dve.wait_ge(T["t_sps"], a + 1)
                    dve.wait_ge(T["t_cps"], a + 1)
                    V.tensor_copy(c_sb[:], bank[0][:, 384:384 + HEADS]).then_inc(T["t_csb"], 1)
                    step("t_var", a, V.tensor_tensor_reduce(out=dots[:], in0=bank[0][:, P:P + A1], in1=patches[:],
                                                            scale=1.0, scalar=0.0, op0=ALU.mult, op1=ALU.add,
                                                            accum_out=varsum[:]))
                    V.tensor_scalar(varsum[:], varsum[:], s00e[:, 0:1], None, ALU.add).then_inc(T["t_vare"], 1)
                    dve.wait_ge(T["t_rstd"], a + 1)
                    V.tensor_scalar(diag[:], ident[:], rstd[:, 0:1], None, ALU.mult).then_inc(T["t_diag"], 1)
                    V.tensor_scalar(rscale[:], rstd[:], float(DIM) ** -0.5, None, ALU.mult)
                    V.tensor_tensor(rmask[:], rstd[:], mask[:], ALU.mult).then_inc(T["t_rm"], 1)
                if attend:
                    dve.wait_ge(T["t_rps"], a + 1)
                    V.tensor_copy(Rbc[:], bank[0][:, 448:448 + PAD_SEQ]).then_inc(T["t_rbc"], 1)
                    dve.wait_ge(T["t_csb"], a + 1)
                    dve.wait_ge(T["t_scps"], a + 1)
                    step("t_s1", a, V.tensor_tensor(
                        s1[:], bank[2][:, 0:HEADS * PAD_SEQ].rearrange("p (h n) -> p h n", h=HEADS)[:, :, 0:SEQ],
                        c_sb[:].unsqueeze(2).broadcast_to([P, HEADS, SEQ]), ALU.add))
                    dve.wait_ge(T["t_rbc"], a + 1)
                    step("t_s2", a, V.tensor_tensor(
                        s2[:], s1[:], Rbc[:, 0:SEQ].unsqueeze(1).broadcast_to([P, HEADS, SEQ]), ALU.mult))
                    step("t_mx", a, V.reduce_max(mx[:], s2[:], axis=AX.X))
                    dve.wait_ge(T["t_rm"], a + 1)
                    V.tensor_scalar(nmx[:], mx[:], rscale[:, 0:1], -1.0, ALU.mult, ALU.mult).then_inc(T["t_nmx"], 1)
                if ffn:
                    dve.wait_ge(T["t_tanh"], f + 1)
                    V.scalar_tensor_tensor(out=act[:], in0=gate_t[:], scalar=1.0, in1=bank[5][:, 0:HID],
                                           op0=ALU.add, op1=ALU.mult).then_inc(T["t_sact"], 1)
                if attend:
                    dve.wait_ge(T["t_exp"], a + 1)
                    step("t_esi", a, V.reciprocal(winv[:], esum[:]))
                    step("t_winv", a, V.tensor_scalar(winv[:], winv[:], rmask[:, 0:1], None, ALU.mult))
                    for half in range(2):
                        q = slice(half * PAD_SEQ, (half + 1) * PAD_SEQ)
                        ins = V.tensor_tensor(mixw[q, :, half * PAD_SEQ:half * PAD_SEQ + SEQ], ex[q],
                                              winv[q].unsqueeze(2).broadcast_to([PAD_SEQ, HEADS, SEQ]), ALU.mult)
                    ins.then_inc(T["t_mixw"], 1)
                if ffn:
                    dve.wait_ge(T["t_sact"], f + 1)
                    dve.wait_ge(T["t_h3ps"], f + 1)
                    V.scalar_tensor_tensor(out=act[:], in0=bank[6][:, 0:HID], scalar=0.5, in1=act[:],
                                           op0=ALU.mult, op1=ALU.mult).then_inc(T["t_act"], 1)
                    dve.wait_ge(T["t_gps"], f + 1)
                    V.tensor_copy(logits[:, bass.ds(f, 1), :].rearrange("p a e -> p (a e)"),
                                  bank[2][:, 256:256 + EXPERTS]).then_inc(T["t_lg"], 1)
                if attend:
                    dve.wait_ge(T["t_h2ps"], a + 1)
                    V.bn_stats(stats[:], bank[4][:]).then_inc(T["t_stats"], 1)
                    dve.wait_ge(s_const, 1)
                    dve.wait_ge(T["t_stats"], a + 1)
                    step("t_aggr", a, V.bn_aggr(aggr[:], stats[:]))
                    V.tensor_scalar(var2[:], aggr[:, 1:2], EPS, None, ALU.add).then_inc(T["t_var2"], 1)
                    dve.wait_ge(T["t_rstd2"], a + 1)
                    if ffn:
                        dve.wait_ge(s_xnst, 16 * a)
                    V.tensor_scalar(xn[:], bank[4][:], aggr[:, 0:1], rstd2[:, 0:1], ALU.subtract,
                                    ALU.mult).then_inc(T["t_xn"], 1)
                if ffn:
                    dve.wait_ge(T["t_ops"], f + 1)
                    dve.wait_ge(T["t_h2sb"], f + 1)
                    dve.wait_ge(s_accst, 16 * f)
                    V.tensor_tensor(acc[:], bank[5][:], h2[:], ALU.add).then_inc(T["t_acc"], 1)

            token_tile(-1, True, False)
            token_tile(0, True, True)
            with dve.Fori(1, TILES - 1) as i:
                token_tile(i, True, True)
            token_tile(TILES - 1, False, True)

            dve.wait_ge(s_const, 2)

            def bc(col):
                return col.unsqueeze(2).broadcast_to([P, TILES, EXPERTS])
            bias_te = bias_bc[:].unsqueeze(1).broadcast_to([P, TILES, EXPERTS])
            dve.wait_ge(T["t_lg"], TILES)
            link(V.reduce_max(rmx[:], logits[:], axis=AX.X))
            V.tensor_tensor(z[:], logits[:], bc(rmx[:]), ALU.subtract).then_inc(r_ez, 1)
            dve.wait_ge(r_exp, 1)
            link(V.reduce_sum(rsum[:], prob[:], axis=AX.X))
            link(V.reciprocal(rsum[:], rsum[:]))
            link(V.tensor_tensor(prob[:], prob[:], bc(rsum[:]), ALU.mult))
            link(V.tensor_tensor(choice[:], prob[:], bias_te, ALU.add))

            def best(v, i, oh, k):
                link(V.reduce_max(v[:], choice[:], axis=AX.X))
                link(V.tensor_tensor(eq[:], choice[:], bc(v[:]), ALU.is_ge))
                link(V.scalar_tensor_tensor(out=eq[:], in0=eq[:], scalar=-float(EXPERTS), in1=iota_e[:],
                                            op0=ALU.mult, op1=ALU.add))
                link(V.tensor_reduce(i[:], eq[:], axis=AX.X, op=ALU.min))
                link(V.tensor_scalar(i[:], i[:], float(EXPERTS), None, ALU.add))
                link(V.tensor_tensor(oh[:], iota_e[:], bc(i[:]), ALU.is_equal))
                link(V.tensor_tensor(tmp[:], oh[:], prob[:], ALU.mult))
                link(V.reduce_sum(prob_k[:, k, :], tmp[:], axis=AX.X))

            best(v1, i1, oh1, 0)
            link(V.scalar_tensor_tensor(out=choice[:], in0=oh1[:], scalar=-3.0e38, in1=choice[:],
                                        op0=ALU.mult, op1=ALU.add))
            best(v2, i2, oh2, 1)
            V.tensor_tensor(M[:], oh1[:], oh2[:], ALU.add).then_inc(r_M, 1)
            dve.wait_ge(r_rank, 1)
            rank_ps = bank[0][:, 0:TE].rearrange("p (t e) -> p t e", t=TILES)
            link(V.tensor_scalar(tmp[:], bank[1][:, 0:TE].rearrange("p (t e) -> p t e", t=TILES), float(DIM), None,
                                 ALU.mult))
            link(V.memset(z[:], 1.0))
            for e in range(EXPERTS):
                last = V.tensor_tensor_scan(incl[:, :, e], z[:, :, e], tmp[:, :, e], 0.0, ALU.mult, ALU.add)
            link(last)
            link(V.tensor_scalar(totals[:], incl[:, TILES - 1, :], float(P - 1), None, ALU.add))
            link(V.tensor_copy(int_e[:], totals[:]))
            link(V.tensor_scalar(int_e[:], int_e[:], LOG_P, None, ALU.logical_shift_right))
            link(V.tensor_copy(ntiles[:], int_e[:]))
            link(V.tensor_tensor_scan(ends[:], z[:, 0, :], ntiles[:], 0.0, ALU.mult, ALU.add))
            link(V.tensor_tensor(starts[:], ends[:], ntiles[:], ALU.subtract))
            link(V.tensor_tensor(incl[:], incl[:], tmp[:], ALU.subtract))
            link(V.tensor_tensor(incl[:], incl[:], rank_ps, ALU.add))
            link(V.scalar_tensor_tensor(out=pos[:], in0=starts[:].unsqueeze(1).broadcast_to([P, TILES, EXPERTS]),
                                        scalar=float(P), in1=incl[:], op0=ALU.mult, op1=ALU.add))
            for k, oh in enumerate((oh1, oh2)):
                link(V.tensor_tensor(tmp[:], oh[:], pos[:], ALU.mult))
                link(V.reduce_sum(pk[:, k, :], tmp[:], axis=AX.X))
            link(V.tensor_copy(int_k[:], pk[:]))
            link(V.tensor_scalar(int_low[:], int_k[:], P - 1, None, ALU.bitwise_and))
            link(V.tensor_copy(low[:], int_low[:]))
            link(V.tensor_scalar(int_k[:], int_k[:], LOG_P, None, ALU.logical_shift_right))
            link(V.tensor_copy(hi[:], int_k[:]))
            link(V.tensor_tensor(val[:], tok_id[:].unsqueeze(1).broadcast_to([P, TOPK, TILES]), low[:], ALU.subtract))
            link(V.tensor_scalar(val[:], val[:], -float(TOKENS), None, ALU.add))
            link(V.tensor_tensor(te_cmp[:], iota_s[0:1, :].unsqueeze(2).broadcast_to([1, SLOT_TILES, EXPERTS]),
                                 ends[0:1, :].unsqueeze(1).broadcast_to([1, SLOT_TILES, EXPERTS]), ALU.is_ge))
            link(V.reduce_sum(te_sum[:], te_cmp[:], axis=AX.X))
            link(V.tensor_scalar(tile_expert[:], te_sum[:], float(EXPERTS - 1), None, ALU.min))

            lowf = low[:].rearrange("p k t -> p (k t)")
            hif, valf, probf = (v[:].rearrange("p k t -> p (k t)") for v in (hi, val, prob_k))
            def onehot_rows(g, b):
                cols = bass.ds((2 * g + b) * CG, CG)
                V.tensor_tensor(hihot[b][:], iota_s[:].unsqueeze(1).broadcast_to([P, CG, SLOT_TILES]),
                                hif[:, cols].unsqueeze(2).broadcast_to([P, CG, SLOT_TILES]),
                                ALU.is_equal).then_inc(r_oh, 1)
                V.tensor_tensor(lowhot[b][:], iota_p[:].unsqueeze(1).broadcast_to([P, CG, P]),
                                lowf[:, cols].unsqueeze(2).broadcast_to([P, CG, P]), ALU.is_equal)
                dve.wait_ge(r_oh, 4 * g + 2 * b + 1)
                V.tensor_tensor(hival[b][:, :, 0:SLOT_TILES], hihot[b][:],
                                valf[:, cols].unsqueeze(2).broadcast_to([P, CG, SLOT_TILES]), ALU.mult)
                V.tensor_tensor(hival[b][:, :, SLOT_TILES:], hihot[b][:],
                                probf[:, cols].unsqueeze(2).broadcast_to([P, CG, SLOT_TILES]),
                                ALU.mult).then_inc(r_oh, 1)

            onehot_rows(0, 0)
            onehot_rows(0, 1)
            with dve.Fori(1, C // (2 * CG)) as g:
                dve.wait_ge(r_ohused, 2 * g)
                onehot_rows(g, 0)
                onehot_rows(g, 1)
            dve.wait_ge(r_list, 1)
            V.tensor_scalar(slot_idx[:], bank[2][:, 0:SLOT_TILES], spare_row[:, 0:1], None, ALU.add)
            V.tensor_copy(slot_score[:], bank[2][:, SLOT_TILES:2 * SLOT_TILES]).then_inc(r_done, 1)

            def gate(t, c):
                j = 2 * t + c
                dve.wait_ge(R["e_gate"], j + 1)
                dve.wait_ge(R["e_h3ps"], j + 1)
                dve.wait_ge(R["e_htps"], j)
                V.scalar_tensor_tensor(out=ract[:], in0=bank[2][:, 0:HID], scalar=score[c][:, 0:1], in1=rgate[:],
                                       op0=ALU.mult, op1=ALU.mult).then_inc(R["e_act"], 1)

            def y_out(j):
                dve.wait_ge(R["e_yps"], j + 1)
                dve.wait_ge(s_scatter, 16 * j)
                V.tensor_copy(y_sb[:], bank[4][:]).then_inc(R["e_ysb"], 1)

            gate(0, 0)
            gate(0, 1)
            y_out(0)
            with dve.Fori(1, SLOT_TILES // 2) as t:
                for c in range(2):
                    gate(t, c)
                    y_out(2 * t + c - 1)
            gate(SLOT_TILES // 2, 0)
            y_out(SLOT_TILES - 2)
            y_out(SLOT_TILES - 1)

        @block.tensor
        def _(pe):
            MM = nc.tensor.matmul

            pe.wait_ge(s_tok, 32)
            pe.wait_ge(s_const, 1)
            for k in range(KT):
                ins = MM(bank[0][:, 0:A1], ones[:], A_T[:, k, :], start=k == 0, stop=k == KT - 1)
            ins.then_inc(s_mean, 1)
            pe.wait_ge(s_cen, 1)
            for k in range(KT):
                MM(bank[1][:, 0:A1], A_T[:, k, 0:P], A_T[:, k, :], start=k == 0, stop=k == KT - 1)
            for k in range(KT):
                ins = MM(bank[2][:, 0:1], ones[:], bc2[:, k:k + 1], start=k == 0, stop=k == KT - 1)
            ins.then_inc(s_sps, 1)
            pe.wait_ge(s_ssb, 1)
            for n in range(3 * HEADS * KT):
                m, db = n // KT, n % KT
                if db == 0:
                    pe.wait_ge(s_qkv[m], 16)
                if n >= 8:
                    pe.wait_ge(s_wae, n - 7)
                for k in range(KT):
                    ins = MM(bank[n % 8][:, 0:A1], qkvT[:, m, k, db * P:(db + 1) * P], A_T[:, k, :],
                             start=k == 0, stop=k == KT - 1)
                ins.then_inc(s_wa, 1)
            pe.wait_ge(s_wae, 3 * HEADS * KT)
            pe.wait_ge(s_fc, 16)
            for h in range(HEADS):
                QA, KA, VA = qkvA[:, h], qkvA[:, HEADS + h], qkvA[:, 2 * HEADS + h]
                if h >= 2:
                    pe.wait_ge(s_gfe, h - 1)
                b = 4 * (h % 2)
                for dst, lhs, rhs in ((bank[b][:, 0:A1], KA[:, :, 0:P], QA[:, :, :]),
                                      (bank[b][:, 256:257], QA[:, :, 0:P], KA[:, :, P:A1]),
                                      (bank[b + 1][0:1, 0:1], QA[:, :, P:A1], KA[:, :, P:A1]),
                                      (bank[b + 2][:], VA[:, :, 0:P], fcT_sb[:])):
                    for k in range(KT):
                        ins = MM(dst, lhs[:, k, :], rhs[:, k, :], start=k == 0, stop=k == KT - 1)
                ins.then_inc(s_gf, 1)
            for k in range(KT):
                ins = MM(bank[3][0:HEADS, :], qkvA[:, 2 * HEADS:3 * HEADS, k, P], fcT_sb[:, k, :],
                         start=k == 0, stop=k == KT - 1)
            ins.then_inc(s_f128, 1)
            pe.wait_ge(s_gfe, HEADS)
            pe.wait_ge(s_folded, 1)
            pe.wait_ge(s_bload, 16 * 7)

            def transpose_patches(a):
                pe.wait_ge(s_patch, 16 * a + 16)
                pe.wait_ge(T["t_rbc"], a)
                nc.tensor.transpose(bank[0][:, 0:P], patches[:, 0:P], ident[:]).then_inc(T["t_pt"], 1)

            def token_tile(i, attend, ffn, more=True):
                a, f = i + 1, i
                if attend:
                    pe.wait_ge(T["t_ptsb"], a + 1)
                    MM(bank[0][:, P:P + A1], PT[:], S[:], start=True, stop=True).then_inc(T["t_sps"], 1)
                    MM(bank[0][:, 384:384 + HEADS], PT[:], g_row[:], start=True, stop=False)
                    MM(bank[0][:, 384:384 + HEADS], ones_row[0:1, :], g00[0:1, :], start=False, stop=True).then_inc(T["t_cps"], 1)
                if ffn:
                    pe.wait_ge(T["t_xn"], f + 1)
                    for k in range(KT):
                        ins = nc.tensor.transpose(bank[7][:, k * P:(k + 1) * P], xn[:, k * P:(k + 1) * P], ident[:])
                    ins.then_inc(T["t_xtps"], 1)
                if attend:
                    for h in range(HEADS):
                        ins = MM(bank[1][:, h * P:(h + 1) * P], GT[:, h, :], PT[:], start=True, stop=True)
                    ins.then_inc(T["t_ups"], 1)
                if ffn:
                    pe.wait_ge(T["t_xtsb"], f + 1)
                    pe.wait_ge(T["t_acc"], f)
                    for k in range(KT):
                        ins = MM(bank[5][:, 0:HID], xnT[:, k, :], sw1_sb[:, k, :], start=k == 0, stop=k == KT - 1)
                    ins.then_inc(T["t_h1ps"], 1)
                if attend:
                    pe.wait_ge(T["t_diag"], a + 1)
                    for half in range(2):
                        q = slice(half * PAD_SEQ, (half + 1) * PAD_SEQ)
                        ins = MM(bank[0][q, 448:448 + PAD_SEQ], ones1[:], diag[:, q], start=True, stop=True)
                    ins.then_inc(T["t_rps"], 1)
                    pe.wait_ge(T["t_usb"], a + 1)
                    if ffn:
                        pe.wait_ge(T["t_lg"], f)
                    for h in range(HEADS):
                        for half in range(2):
                            q = slice(half * PAD_SEQ, (half + 1) * PAD_SEQ)
                            ins = MM(bank[2][q, h * PAD_SEQ:(h + 1) * PAD_SEQ], U[:, h, q], PT[:, q],
                                     start=True, stop=True)
                    ins.then_inc(T["t_scps"], 1)
                if ffn:
                    for k in range(KT):
                        ins = MM(bank[6][:, 0:HID], xnT[:, k, :], sw3_sb[:, k, :], start=k == 0, stop=k == KT - 1)
                    ins.then_inc(T["t_h3ps"], 1)
                    if attend:
                        pe.wait_ge(T["t_s1"], a + 1)
                    for k in range(KT):
                        ins = MM(bank[2][:, 256:256 + EXPERTS], xnT[:, k, :], gw_sb[:, k, :], start=k == 0, stop=k == KT - 1)
                    ins.then_inc(T["t_gps"], 1)
                if attend:
                    pe.wait_ge(T["t_mixw"], a + 1)
                    MM(bank[3][:, 0:HEADS * P], patches[:, 0:P], mixw[:].rearrange("p h t -> p (h t)"),
                       start=True, stop=True)
                    for h in range(HEADS):
                        ins = MM(bank[1][0:HEADS, HEADS * P:(HEADS + 1) * P], onehot_h[:, h, :], mixw[:, h, :],
                                 start=h == 0, stop=h == HEADS - 1)
                    ins.then_inc(T["t_yps"], 1)
                    pe.wait_ge(T["t_h2sb"], a)
                    MM(bank[4][:], PT[:], tokWT_sb[:], start=True, stop=False)
                    pe.wait_ge(T["t_ysb"], a + 1)
                if ffn:
                    pe.wait_ge(T["t_act"], f + 1)
                    for k in range(KT):
                        ins = nc.tensor.transpose(bank[3][0:HB, k * P:(k + 1) * P], act[:, k * HB:(k + 1) * HB], ident[:])
                    ins.then_inc(T["t_htps"], 1)
                if attend:
                    for h in range(HEADS):
                        MM(bank[4][:], YT[:, h, :], F[:, h, :], start=False, stop=False)
                    MM(bank[4][:], y0[0:HEADS + 2, :], tail[:], start=False, stop=True).then_inc(T["t_h2ps"], 1)
                    if more:
                        transpose_patches(a + 1)
                if ffn:
                    pe.wait_ge(T["t_htsb"], f + 1)
                    for k in range(KT):
                        ins = MM(bank[5][:], hT[0:HB, k, :], sw2_sb[:, k, :], start=k == 0, stop=k == KT - 1)
                    ins.then_inc(T["t_ops"], 1)

            transpose_patches(0)
            token_tile(-1, True, False)
            token_tile(0, True, True)
            with pe.Fori(1, TILES - 2) as i:
                token_tile(i, True, True)
            token_tile(TILES - 2, True, True, more=False)
            token_tile(TILES - 1, False, True)

            pe.wait_ge(r_M, 1)
            Mf = M[:].rearrange("p t e -> p (t e)")
            MM(bank[0][:, 0:TE], tri[:], Mf, start=True, stop=True)
            MM(bank[1][:, 0:TE], ones[:], Mf, start=True, stop=True).then_inc(r_rank, 1)

            def list_group(g, b, first, last):
                pe.wait_ge(r_oh, 4 * g + 2 * b + 2)
                for c in range(CG):
                    ins = MM(bank[2][:, 0:2 * SLOT_TILES], lowhot[b][:, c, :], hival[b][:, c, :],
                             start=first and c == 0, stop=last and c == CG - 1)
                ins.then_inc(r_ohused, 1)
                return ins

            G = C // (2 * CG)
            list_group(0, 0, True, False)
            list_group(0, 1, False, False)
            with pe.Fori(1, G - 1) as g:
                list_group(g, 0, False, False)
                list_group(g, 1, False, False)
            list_group(G - 1, 0, False, False)
            list_group(G - 1, 1, False, True)
            nc.tensor.transpose(bank[3][:, 0:P], ident[:], ident[:]).then_inc(r_list, 1)
            pe.wait_ge(r_done, 1)

            def transpose_rows(t, c):
                j = 2 * t + c
                pe.wait_ge(s_gather[c], 16 * t + 16)
                pe.wait_ge(R["e_xsb"], j)
                for k in range(KT):
                    ins = nc.tensor.transpose(bank[0][:, k * P:(k + 1) * P], xg[c][:, k * P:(k + 1) * P], ident[:])
                ins.then_inc(R["e_xps"], 1)

            def up(j, e, third, dst, done):
                for k in range(KT):
                    o = e * W_WORDS + (third * KT + k) * HID
                    ins = MM(dst[:, 0:HID], xgT[:, k, :], experts[:, bass.ds(o, HID)], start=k == 0, stop=k == KT - 1)
                ins.then_inc(done, 1)

            def transpose_hidden(j):
                pe.wait_ge(R["e_act"], j + 1)
                for k in range(KT):
                    ins = nc.tensor.transpose(bank[3][0:HB, k * P:(k + 1) * P], ract[:, k * HB:(k + 1) * HB], ident[:])
                ins.then_inc(R["e_htps"], 1)

            def down(j, e):
                pe.wait_ge(R["e_htsb"], j + 1)
                pe.wait_ge(R["e_ysb"], j)
                for k in range(KT):
                    o = e * W_WORDS + 2 * KT * HID + k * DIM
                    ins = MM(bank[4][:], rhT[0:HB, k, :], experts[0:HB, bass.ds(o, DIM)], start=k == 0, stop=k == KT - 1)
                ins.then_inc(R["e_yps"], 1)

            def expert_of(j):
                return pe.value_load(tile_expert[0:1, bass.ds(j, 1)], min_val=0, max_val=EXPERTS - 1)

            def slot_tile(t, c, before=True, after=True):
                j = 2 * t + c
                e = expert_of(j)
                pe.wait_ge(s_expert, 48 * e + 48)
                pe.wait_ge(R["e_xsb"], j + 1)
                if before:
                    pe.wait_ge(R["e_act"], j)
                up(j, e, 0, bank[1], R["e_h1ps"])
                if before:
                    transpose_hidden(j - 1)
                up(j, e, 1, bank[2], R["e_h3ps"])
                if after:
                    transpose_rows(t + c, 1 - c)
                if before:
                    down(j - 1, expert_of(j - 1))

            transpose_rows(0, 0)
            slot_tile(0, 0, before=False)
            slot_tile(0, 1)
            with pe.Fori(1, SLOT_TILES // 2) as t:
                slot_tile(t, 0)
                slot_tile(t, 1)
            slot_tile(SLOT_TILES // 2, 0, after=False)
            transpose_hidden(SLOT_TILES - 1)
            down(SLOT_TILES - 1, expert_of(SLOT_TILES - 1))


def kernel(x, L0_tok_W, L0_tok_b, L0_attn_Wq, L0_attn_Wk, L0_attn_Wv, L0_attn_fc_w, L0_attn_fc_b, L0_ffn_gate_w,
           L0_ffn_w1, L0_ffn_w2, L0_ffn_w3, L0_ffn_sw1, L0_ffn_sw2, L0_ffn_sw3, L0_ffn_expert_bias):
    import numpy as np
    import concourse.bacc as bacc
    from concourse.bass_utils import run_bass_kernel_spmd

    def t(a):
        return np.ascontiguousarray(np.swapaxes(np.asarray(a), -1, -2))

    arrays = {
        "x": np.ascontiguousarray(np.asarray(x).reshape(-1)),
        "tokWT": t(L0_tok_W), "tokW": np.asarray(L0_tok_W), "tokb": np.asarray(L0_tok_b),
        "WqT": t(L0_attn_Wq), "WkT": t(L0_attn_Wk), "WvT": t(L0_attn_Wv), "fcT": t(L0_attn_fc_w),
        "fcb": np.asarray(L0_attn_fc_b), "gate_w": np.asarray(L0_ffn_gate_w),
        "w1": np.asarray(L0_ffn_w1), "w2": np.asarray(L0_ffn_w2), "w3": np.asarray(L0_ffn_w3),
        "sw1": np.asarray(L0_ffn_sw1), "sw2": np.asarray(L0_ffn_sw2), "sw3": np.asarray(L0_ffn_sw3),
        "ebias": np.asarray(L0_ffn_expert_bias),
    }
    nc = bacc.Bacc("TRN2", target_bir_lowering=False, num_devices=1)
    args = [nc.dram_tensor(f"in_{n}", a.shape, mybir.dt.from_np(a.dtype), kind="ExternalInput").ap()
            for n, a in arrays.items()]
    out = nc.dram_tensor("rows_out", (TOKENS + P, DIM), mybir.dt.float32, kind="ExternalOutput").ap()
    audio_tower(nc, *args, out)
    r = run_bass_kernel_spmd(nc, [{f"in_{n}": a for n, a in arrays.items()}], core_ids=[0])
    rows = r.results[0]["rows_out"]
    return rows[:TOKENS].reshape(BATCH, PAD_SEQ, DIM)[:, :SEQ]
```

```python
import concourse.bass as bass
from concourse import mybir
from contextlib import ExitStack

BATCH, SAMPLES = 64, 4096
PATCH, STRIDE = 128, 64
SEQ = (SAMPLES - PATCH) // STRIDE + 1
PAD_SEQ = 64
DIM, HEADS, HID, EXPERTS, TOPK = 512, 3, 448, 8, 2
P, LOG_P = 128, 7
TOKENS = BATCH * PAD_SEQ
TILES = TOKENS // P
KT = DIM // P
FULL = HID // P
REST = HID - FULL * P
assert REST * 2 == P and FULL + 1 == KT
SLOT_TILES = (BATCH * SEQ * TOPK + TOPK * (P - 1) + (EXPERTS - TOPK) * P) // P
assert SLOT_TILES % 2 == 0
EPS = 1e-5
A1 = PATCH + 1
BLK = 2 * HID + DIM
CHUNKS = EXPERTS * KT
assert CHUNKS == TILES
W_WORDS = KT * BLK
RING_PLACES = 4
EXPERT_DMAS = (2, 5)
GW = HID + EXPERTS


def audio_tower(nc, x, tokWT, tokW, tokb, WqT, WkT, WvT, fcT, fcb, wpack, swpack, ebias, out):
    f32, f32r, u32 = mybir.dt.float32, mybir.dt.float32r, mybir.dt.uint32
    ALU, ACT, AX = mybir.AluOpType, mybir.ActivationFunctionType, mybir.AxisListType
    ctx = ExitStack()
    with ctx:
        def sb(name, shape, dt=f32):
            return ctx.enter_context(nc.sbuf_tensor(name, shape, dt))

        def sem(name):
            return ctx.enter_context(nc.semaphore(name))

        xn_dram = nc.dram_tensor("xn_rows", [TOKENS + P, DIM], f32, kind="Internal").ap()

        parts_dram = nc.dram_tensor("expert_parts", [CHUNKS, P, 2 * BLK], f32, kind="Internal").ap()

        def words_of(tensor):
            place = [0]

            def words(n, *dims, parts=P):
                a = place[0]
                place[0] += n
                assert place[0] <= tensor.shape[1], (place[0], tensor.shape)
                v = tensor[0:parts, a:a + n]
                if len(dims) == 2:
                    v = v.rearrange("p (a b) -> p a b", a=dims[0])
                if len(dims) == 3:
                    v = v.rearrange("p (a b c) -> p a b c", a=dims[0], b=dims[1])
                return v
            return words

        PLACE = 2 * W_WORDS
        SW_WORDS = KT * GW + KT * HID + KT * DIM
        assert 2 * SW_WORDS >= PLACE
        ring_at = (nc.sbuf_base + 31) // 32 * 32
        ring = sb("ring", [P, RING_PLACES * PLACE], f32r)
        taken = [0]

        def in_ring(n, *tensors):
            word = taken[0]
            taken[0] += (n + 7) // 8 * 8
            assert taken[0] <= RING_PLACES * PLACE
            views = [nc.alloc_sbuf_tensor_at(name, shape, dt, offset=ring_at + 4 * (word + (skip[0] if skip else 0)))
                     for name, shape, dt, *skip in tensors]
            return views[0] if len(views) == 1 else views

        fold = in_ring(2 * PLACE, ("fold", [P, 2 * PLACE], f32))
        shared, scratch = in_ring(2 * SW_WORDS, ("shared", [P, 2 * SW_WORDS], f32r),
                                  ("scratch", [P, 2 * SW_WORDS], f32))
        words = words_of(fold)
        qkvT = words(3 * HEADS * KT * DIM, 3 * HEADS, KT, DIM)
        fcT_sb = words(KT * DIM, KT, DIM)
        sw_raw = fold[:, 0:KT * GW + KT * HID + KT * DIM]
        assert sw_raw.shape[1] <= HEADS * KT * DIM

        FOLDED = 3 * HEADS * KT * A1 + KT * A1 + A1 + KT
        cutting, blk_hl = in_ring(FOLDED, ("cutting", [P, FOLDED], f32), ("blk_hl", [P, 2, BLK], f32r, BLK))
        assert FOLDED >= 3 * BLK
        words = words_of(cutting)
        qkvA = words(3 * HEADS * KT * A1, 3 * HEADS, KT, A1)
        A_T = words(KT * A1, KT, A1)
        A_mean = words(A1)
        bc2 = words(KT)
        blk_raw = cutting[:, 0:BLK]
        words = words_of(cutting[:, 3 * BLK:])
        iota_e = words(TILES * EXPERTS, TILES, EXPERTS)
        bias_bc = words(EXPERTS)
        tri, iota_p = words(P), words(P)
        iota_s = words(SLOT_TILES)
        spare_row, spare_off, rconst_done = words(1), words(1), words(1)
        tok_id = words(TILES)

        def shared_part(half):
            o = half * SW_WORDS
            return (shared[:, o:o + KT * GW].rearrange("p (k h) -> p k h", k=KT),
                    shared[:, o + KT * GW:o + KT * (GW + HID)].rearrange("p (k h) -> p k h", k=KT),
                    shared[:, o + KT * (GW + HID):o + SW_WORDS].rearrange("p (k d) -> p k d", k=KT))
        sw1g_hl, sw3_hl, sw2_hl = zip(shared_part(0), shared_part(1))

        F_hl, scratch_F = in_ring(2 * HEADS * DIM, ("F_hl", [P, 2, HEADS, DIM], f32r),
                                  ("scratch_F", [P, 2 * HEADS * DIM], f32))
        tokWT_hl = in_ring(2 * DIM, ("tokWT_hl", [P, 2, DIM], f32r))
        TAIL = HEADS + 2
        tail = sb("tail", [64 + TAIL, DIM], f32r)
        y0 = sb("y0", [64 + TAIL, P], f32r)
        small = sb("small", [P, PATCH + 3 * P + A1 + 3 * HEADS + 1 + 2 * A1 + P + 4 + 2 * P + 64 + 5 * HEADS + 10 + 9 + 1 + 64 + P + 8])
        words = words_of(small)
        GT = words(HEADS * P, HEADS, P)
        g_col = words(HEADS)
        g00 = words(HEADS, parts=1)
        g00_bc = words(HEADS)
        S_row = words(A1 + HEADS)
        S = S_row[:, 0:A1]
        g_row = S_row[:, A1:]
        s00e = words(1)
        patches = words(A1)
        dots = words(A1)
        next_patches = words(PATCH)
        PT = words(P)
        varsum, rstd, rscale, rmask = words(1), words(1), words(1), words(1)
        diag = words(P)
        c_sb = words(HEADS)
        Rbc = words(PAD_SEQ)
        mx, nmx, esum, winv = words(HEADS), words(HEADS), words(HEADS), words(HEADS)
        stats, aggr, var2, rstd2 = words(6), words(2), words(1), words(1)
        neg_half = words(1)
        onehot_h = words(HEADS * HEADS, HEADS, HEADS)
        mask = words(1)
        ones1 = words(PAD_SEQ)
        ones_row = words(P, parts=1)
        PT_hl = sb("PT_hl", [P, 2, P], f32r)
        U = in_ring(HEADS * P, ("U", [P, HEADS, P], f32))
        s1 = in_ring(HEADS * SEQ, ("s1", [P, HEADS, SEQ], f32))
        ex = sb("ex", [P, HEADS, SEQ])
        mixw = in_ring(HEADS * P, ("mixw", [P, HEADS, P], f32))
        YT_hl = in_ring(2 * HEADS * P, ("YT_hl", [P, 2, HEADS, P], f32r))
        h2 = sb("h2", [P, DIM])
        xn = sb("xn", [P, DIM])
        xnT_hl = sb("xnT_hl", [P, 2, KT, P], f32r)
        gate_t = sb("gate_t", [P, HID])
        act = sb("act", [P, HID + REST])
        hT_hl = sb("hT_hl", [P, 2, KT, P], f32r)
        acc = sb("acc", [P, DIM])
        tail_raw = acc[0:TAIL, :]
        tokWT_raw = xn

        ident = sb("ident", [P, P])
        ones = sb("ones", [P, P])
        logits = sb("logits", [P, TILES, EXPERTS])
        slot_idx = sb("slot_idx", [P, SLOT_TILES], u32)
        slot_score = sb("slot_score", [P, SLOT_TILES])
        tile_expert = sb("tile_expert", [1, SLOT_TILES], u32)
        tile_place = sb("tile_place", [1, SLOT_TILES], u32)
        first_tile = sb("first_tile", [1, EXPERTS], u32)

        g_idx = [sb(f"g_idx{c}", [P, 1], u32) for c in range(2)]
        s_idx = sb("s_idx", [P, 1], u32)
        score = [sb(f"score{c}", [P, 1]) for c in range(2)]
        xg = [xn, h2]
        xgT_hl, rgate, ract, rhT_hl, y_sb = xnT_hl, gate_t, act, hT_hl, acc

        words = words_of(scratch_F)
        TE = TILES * EXPERTS

        def te():
            return words(TE, TILES, EXPERTS)
        z, prob, choice, eq, oh1, oh2, M, tmp = (te() for _ in range(8))
        rmx, rsum, v1, i1, v2, i2 = (words(TILES) for _ in range(6))
        C = TOPK * TILES
        prob_k = words(C, TOPK, TILES)
        words = words_of(scratch)
        incl, pos = te(), te()
        pk, low, hi, val = (words(C, TOPK, TILES) for _ in range(4))
        totals, ntiles, ends, starts = (words(EXPERTS) for _ in range(4))
        int_e = words(EXPERTS).bitcast(u32)
        int_k, int_low = (words(C).bitcast(u32).rearrange("p (a b) -> p a b", a=TOPK) for _ in range(2))
        CG = 4
        LB = 4
        G = C // (LB * CG)
        lowhot = [words(CG * P, CG, P) for _ in range(LB)]
        hihot = [words(CG * SLOT_TILES, CG, SLOT_TILES) for _ in range(LB)]
        hival = [words(CG * 2 * SLOT_TILES, CG, 2 * SLOT_TILES) for _ in range(LB)]
        te_cmp = words(SLOT_TILES * EXPERTS, SLOT_TILES, EXPERTS, parts=1)
        te_sum, te_place, te_turn = (words(SLOT_TILES, parts=1) for _ in range(3))

        bank = [ctx.enter_context(nc.psum_tensor(f"bank{i}", [P, DIM], f32)) for i in range(8)]

        s_tok, s_fc = sem("s_tok"), sem("s_fc")
        s_qkv = [sem(f"s_qkv{m}") for m in range(3 * HEADS)]
        s_bload, s_patch, s_plast = sem("s_bload"), sem("s_patch"), sem("s_plast")
        s_sw = sem("s_sw")
        s_raw, s_cut = sem("s_raw"), sem("s_cut")
        c_hi, c_lo = sem("c_hi"), sem("c_lo")
        w_hi, w_lo = sem("w_hi"), sem("w_lo")
        s_F, w_Fh, w_F = sem("s_F"), sem("w_Fh"), sem("w_F")
        s_expert = [sem(f"s_expert{b}") for b in range(2)]
        s_zrow, s_xnst, s_accst = sem("s_zrow"), sem("s_xnst"), sem("s_accst")
        s_gather, s_scatter = [sem(f"s_gather{c}") for c in range(2)], sem("s_scatter")
        s_issue = sem("s_issue")
        s_ones, s_bias = sem("s_ones"), sem("s_bias")
        s_const = sem("s_const")
        s_pc = sem("s_pc")
        s_dv = sem("s_dv")
        s_mean, s_cen, s_sps = sem("s_mean"), sem("s_cen"), sem("s_sps")
        s_ssb, s_wa, s_wae, s_gf, s_gfe = (sem(n) for n in ("s_ssb", "s_wa", "s_wae", "s_gf", "s_gfe"))
        s_f128, s_folded = sem("s_f128"), sem("s_folded")
        names = ("t_xta t_patch t_y0ps t_y0 t_vare t_var2 t_tanh t_ptlo t_ylo t_xlo t_hlo t_pt t_ptsb "
                 "t_sps t_ups t_var t_rstd t_diag t_usb t_csb t_rps t_rbc t_scps t_s1 t_mx t_nmx "
                 "t_exp t_rm t_esi t_winv t_mixw t_yps t_ysb t_h2ps t_stats t_aggr t_rstd2 t_xn t_h2sb t_xtps t_xtsb "
                 "t_lg t_h1ps t_h3ps t_sact t_act t_htps t_htsb t_ops t_acc").split()
        T = {n: sem(n) for n in names}
        r_exp, r_ez, r_M, r_rank, r_oh, r_hival, r_hiprob, r_ohused, r_list, r_done = (
            sem(n) for n in ("r_exp", "r_ez", "r_M", "r_rank", "r_oh", "r_hival", "r_hiprob", "r_ohused", "r_list", "r_done"))
        names = "e_gidx e_idx e_sidx e_xps e_xsb e_h1ps e_h3ps e_gate e_act e_htps e_htsb e_yps e_ysb e_xlo e_hlo".split()
        R = {n: sem(n) for n in names}

        block = ctx.enter_context(nc.Block())

        out_t = out[0:TOKENS, :].rearrange("(t p) d -> t p d", p=P)
        xn_t = xn_dram[0:TOKENS, :].rearrange("(t p) d -> t p d", p=P)

        def part(hl, half):
            return hl[:, half].bitcast(f32)

        def patch_rows(row, n):
            return bass.AP(tensor=x.tensor, offset=row * STRIDE, ap=[[STRIDE, n], [1, PATCH]])

        @block.sync
        def _(sp):
            sp.dma_start(A_T[:, :, 0:PATCH], tokW.rearrange("(k p) q -> p k q", p=P)).then_inc(s_tok, 16)
            with nc.allow_non_contiguous_dma(reason="512 words of bias, one in a channel's partition"):
                sp.dma_start(A_T[:, :, PATCH:A1], tokb.rearrange("(k p a) -> p k a", p=P, a=1)).then_inc(s_tok, 16)
            for m, w in enumerate((WqT, WkT, WvT)):
                for h in range(HEADS):
                    sp.dma_start(qkvT[:, m * HEADS + h], w[h].rearrange("(k p) d -> p k d", p=P)).then_inc(
                        s_qkv[m * HEADS + h], 16)
            sp.dma_start(fcT_sb[:], fcT.rearrange("(k p) o -> p k o", p=P)).then_inc(s_fc, 16)
            sp.dma_start(tokWT_raw[:], tokWT[:, :]).then_inc(s_bload, 16)
            sp.dma_start(tail_raw[HEADS:HEADS + 1, :], tokb.rearrange("(a d) -> a d", a=1)).then_inc(s_bload, 16)
            sp.dma_start(tail_raw[HEADS + 1:TAIL, :], fcb.rearrange("(a d) -> a d", a=1)).then_inc(s_bload, 16)
            sp.wait_ge(s_wa, HEADS * KT)
            sp.dma_start(sw_raw, swpack[:, :]).then_inc(s_sw, 16)

            def patches_in(i):
                sp.wait_ge(T["t_pt"], i)
                sp.wait_ge(T["t_patch"], i)
                sp.dma_start(next_patches, bass.AP(tensor=x.tensor, offset=i * (P * STRIDE),
                                                   ap=[[STRIDE, P], [1, PATCH]])).then_inc(s_patch, 16)

            def store_xn(i):
                sp.wait_ge(T["t_xn"], i + 1)
                sp.dma_start(xn_t[bass.ds(i, 1)].rearrange("a p d -> (a p) d"), xn[:]).then_inc(s_xnst, 16)

            def store_acc(i):
                sp.wait_ge(T["t_acc"], i + 1)
                sp.dma_start(out_t[bass.ds(i, 1)].rearrange("a p d -> (a p) d"), acc[:]).then_inc(s_accst, 16)

            def block_in(i):
                sp.wait_ge(c_lo, i)
                sp.dma_start(blk_raw, wpack[bass.ds(i, 1)].rearrange("a p w -> (a p) w")).then_inc(s_raw, 16)

            def parts_out(i):
                sp.wait_ge(c_lo, i + 1)
                sp.dma_start(parts_dram[bass.ds(i, 1)].rearrange("a p w -> (a p) w"),
                             blk_hl[:].bitcast(f32).rearrange("p h w -> p (h w)")).then_inc(s_cut, 16)

            sp.dma_start(next_patches, patch_rows(0, P)).then_inc(s_patch, 16)
            sp.wait_ge(s_folded, 1)
            sp.wait_ge(s_F, HEADS)
            sp.wait_ge(w_lo, 4)
            sp.dma_start(blk_raw, wpack[0]).then_inc(s_raw, 16)
            patches_in(1)
            store_xn(0)
            with sp.Fori(0, TILES - 3) as i:
                patches_in(i + 2)
                parts_out(i)
                block_in(i + 1)
                store_xn(i + 1)
                store_acc(i)
            last = (TILES - 1) * P
            sp.wait_ge(T["t_pt"], TILES - 1)
            sp.wait_ge(T["t_patch"], TILES - 1)
            sp.dma_start(next_patches[0:P - 1, :], patch_rows(last, P - 1)).then_inc(s_plast, 16)
            sp.wait_ge(s_plast, 16)
            sp.dma_start(next_patches[P - 1:P, :], patch_rows(last + P - 2, 1)).then_inc(s_patch, 16)
            parts_out(TILES - 3)
            block_in(TILES - 2)
            store_xn(TILES - 2)
            store_acc(TILES - 3)
            parts_out(TILES - 2)
            block_in(TILES - 1)
            store_xn(TILES - 1)
            store_acc(TILES - 2)
            parts_out(TILES - 1)
            store_acc(TILES - 1)
            sp.wait_ge(s_cut, 16 * CHUNKS)

            def load_expert(e):
                for k in range(KT):
                    b = k % 2
                    before = 16 * EXPERT_DMAS[b] * e + (16 if k >= 2 else 0)
                    if before > 0:
                        sp.wait_ge(s_expert[b], before)
                    o = (e % RING_PLACES) * PLACE + k * 2 * BLK
                    src = parts_dram[e * KT + k]

                    def part_in(p0, p1, to, a, n):
                        sp.dma_start(ring[p0:p1, o + to:o + to + n].bitcast(f32), src[p0:p1, a:a + n]).then_inc(
                            s_expert[b], 16)
                    if k < FULL:
                        part_in(0, P, 0, 0, 2 * BLK)
                    else:
                        part_in(0, REST, 0, 0, 2 * BLK)
                        part_in(REST, P, 0, 0, 2 * HID)
                        part_in(REST, P, 2 * HID, BLK + 2 * HID, DIM)
                        part_in(REST, P, BLK, BLK, 2 * HID)

            load_expert(0)
            load_expert(1)
            sp.wait_ge(r_done, 1)
            for c in range(2):
                sp.wait_ge(s_gather[c], 16)
            load_expert(2)
            load_expert(3)
            for e in range(RING_PLACES, EXPERTS):
                sp.wait_ge(R["e_yps"], sp.value_load(first_tile[0:1, e - 3:e - 2], min_val=1,
                                                     max_val=SLOT_TILES + 1))
                load_expert(e)

        @block.gpsimd
        def _(pool):
            n = [0]

            def link(ins):
                n[0] += 1
                ins.then_inc(s_pc, 1)
                pool.wait_ge(s_pc, n[0])

            nc.gpsimd.memset(ones[:], 1.0 / DIM).then_inc(s_ones, 1)
            link(nc.gpsimd.memset(ident[:], 0.0))
            link(nc.gpsimd.affine_select(out=ident[:], in_=ident[:], compare_op=ALU.not_equal, fill=1.0,
                                         base=0, pattern=[[-1, P]], channel_multiplier=1))
            link(nc.gpsimd.memset(patches[:, PATCH:A1], 2.0))
            link(nc.gpsimd.memset(mixw[:], 0.0))
            link(nc.gpsimd.memset(ones_row[:], 1.0))
            link(nc.gpsimd.memset(neg_half[:], -0.5))
            link(nc.gpsimd.memset(onehot_h[:], 0.0))
            for h in range(HEADS):
                link(nc.gpsimd.memset(onehot_h[:, h, h:h + 1], 1.0))
            link(nc.gpsimd.memset(y0[:].bitcast(f32), 0.0))
            link(nc.gpsimd.memset(y0[0:TAIL, :].bitcast(f32), 1.0))
            link(nc.gpsimd.memset(y0[32:32 + TAIL, :].bitcast(f32), 1.0))
            link(nc.gpsimd.memset(tail[:].bitcast(f32), 0.0))
            link(nc.gpsimd.memset(mask[:], 1.0))
            for spare in (PAD_SEQ - 1, P - 1):
                link(nc.gpsimd.affine_select(out=mask[:], in_=mask[:], compare_op=ALU.not_equal, fill=0.0,
                                             base=-spare, pattern=[[0, 1]], channel_multiplier=1))
            link(nc.gpsimd.memset(h2[:], 0.0))
            pool.dma_start(xn_dram[TOKENS:TOKENS + P, :], h2[:]).then_inc(s_zrow, 16)
            pool.dma_start(out[TOKENS:TOKENS + P, :], h2[:]).then_inc(s_zrow, 16)
            nc.gpsimd.memset(ones1[:], 1.0).then_inc(s_const, 1)

            def routing_constants():
                pool.wait_ge(s_folded, 1)
                pool.wait_ge(s_F, HEADS)
                link(nc.gpsimd.iota(iota_e[:], pattern=[[0, TILES], [1, EXPERTS]], base=0, channel_multiplier=0,
                                    allow_small_or_imprecise_dtypes=True))
                link(nc.gpsimd.iota(iota_p[:], pattern=[[1, P]], base=0, channel_multiplier=0,
                                    allow_small_or_imprecise_dtypes=True))
                link(nc.gpsimd.iota(iota_s[:], pattern=[[1, SLOT_TILES]], base=0, channel_multiplier=0,
                                    allow_small_or_imprecise_dtypes=True))
                link(nc.gpsimd.iota(spare_row[:], pattern=[[0, 1]], base=TOKENS, channel_multiplier=1,
                                    allow_small_or_imprecise_dtypes=True))
                link(nc.gpsimd.iota(tok_id[:], pattern=[[P, TILES]], base=0, channel_multiplier=1,
                                    allow_small_or_imprecise_dtypes=True))
                link(nc.gpsimd.memset(tri[:], 1.0))
                link(nc.gpsimd.affine_select(out=tri[:], in_=tri[:], compare_op=ALU.is_gt, fill=0.0,
                                             base=0, pattern=[[1, P]], channel_multiplier=-1))
                link(nc.gpsimd.tensor_tensor(tri[:], tri[:], mask[:, 0:1].broadcast_to([P, P]), ALU.mult))
                link(nc.gpsimd.memset(spare_off[:], 0.0))
                for spare in (PAD_SEQ - 1, P - 1):
                    link(nc.gpsimd.affine_select(out=spare_off[:], in_=spare_off[:], compare_op=ALU.not_equal,
                                                 fill=float(P), base=-spare, pattern=[[0, 1]], channel_multiplier=1))
                pool.dma_start(bias_bc[:], ebias.rearrange("(a e) -> a e", a=1).broadcast_to([P, EXPERTS])).then_inc(s_bias, 16)
                nc.gpsimd.memset(rconst_done[:], 0.0).then_inc(s_const, 1)

            def token_tile(i, attend, ffn, more=True):
                a, f = i + 1, i
                if attend:
                    pool.wait_ge(T["t_vare"], a + 1)
                    nc.gpsimd.tensor_tensor(rstd[:], varsum[:], neg_half[:], ALU.pow).then_inc(T["t_rstd"], 1)
                if not ffn:
                    routing_constants()
                if ffn:
                    pool.wait_ge(c_hi, f + 1)
                    nc.gpsimd.tensor_tensor(blk_hl[:, 1, :], blk_raw, part(blk_hl, 0), ALU.subtract).then_inc(c_lo, 1)
                if more:
                    pool.wait_ge(T["t_yps"], a + 1)
                    pool.wait_ge(s_patch, 16 * (a + 2))
                    pool.sem_inc(s_issue, 1)
                    nc.gpsimd.tensor_copy(patches[:, 0:PATCH], next_patches).then_inc(T["t_patch"], 1)
                if attend:
                    pool.wait_ge(T["t_var2"], a + 1)
                    nc.gpsimd.tensor_tensor(rstd2[:], var2[:], neg_half[:], ALU.pow).then_inc(T["t_rstd2"], 1)

            pool.wait_ge(s_patch, 16)
            nc.gpsimd.tensor_copy(patches[:, 0:PATCH], next_patches).then_inc(T["t_patch"], 1)
            token_tile(-1, True, False)
            with pool.Fori(0, TILES - 2) as i:
                token_tile(i, True, True)
            token_tile(TILES - 2, True, True, more=False)
            token_tile(TILES - 1, False, True, more=False)
            pool.wait_ge(T["t_acc"], TILES)

            valf = val[:].rearrange("p k t -> p (k t)")

            def hival_rows(g, b):
                pool.wait_ge(r_oh, LB * g + b + 1)
                nc.gpsimd.tensor_tensor(
                    hival[b][:, :, 0:SLOT_TILES], hihot[b][:],
                    valf[:, bass.ds((LB * g + b) * CG, CG)].unsqueeze(2).broadcast_to([P, CG, SLOT_TILES]),
                    ALU.mult).then_inc(r_hival, 1)

            for b in range(LB):
                hival_rows(0, b)
            with pool.Fori(1, G) as g:
                for b in range(LB):
                    pool.wait_ge(r_ohused, LB * (g - 1) + b + 1)
                    hival_rows(g, b)
            pool.wait_ge(s_xnst, 16 * TILES)
            pool.wait_ge(s_accst, 16 * TILES)
            pool.wait_ge(r_done, 1)

            def gather(t, c, first=False):
                j = 2 * t + c
                if not first:
                    pool.wait_ge(R["e_xps"], j - 1)
                nc.gpsimd.tensor_copy(g_idx[c][:], slot_idx[:, bass.ds(j, 1)]).then_inc(R["e_gidx"], 1)
                pool.wait_ge(R["e_gidx"], j + 1)
                pool.sem_inc(s_issue, 1)
                pool.indirect_dma_start(out=xg[c][:], out_offset=None, in_=xn_dram[:, :],
                                        in_offset=bass.IndirectOffsetOnAxis(ap=g_idx[c][:, 0:1], axis=0)
                                        ).then_inc(s_gather[c], 16)

            def scores(t, c, first=False):
                j = 2 * t + c
                if not first:
                    pool.wait_ge(R["e_act"], j - 1)
                nc.gpsimd.tensor_copy(score[c][:], slot_score[:, bass.ds(j, 1)]).then_inc(R["e_idx"], 1)

            def scatter(j, first=False):
                if not first:
                    pool.wait_ge(s_scatter, 16 * j)
                nc.gpsimd.tensor_copy(s_idx[:], slot_idx[:, bass.ds(j, 1)]).then_inc(R["e_sidx"], 1)
                pool.wait_ge(R["e_sidx"], j + 1)
                pool.wait_ge(R["e_ysb"], j + 1)
                pool.sem_inc(s_issue, 1)
                pool.indirect_dma_start(out=out[:, :], out_offset=bass.IndirectOffsetOnAxis(ap=s_idx[:, 0:1], axis=0),
                                        in_=y_sb[:], in_offset=None, compute_op=ALU.add).then_inc(s_scatter, 16)

            gather(0, 0, first=True)
            gather(0, 1, first=True)
            scores(0, 0, first=True)
            scores(0, 1, first=True)
            gather(1, 0)
            gather(1, 1)
            scores(1, 0)
            scatter(0, first=True)
            with pool.Fori(2, SLOT_TILES // 2) as t:
                gather(t, 0)
                scores(t - 1, 1)
                scatter(2 * t - 3)
                gather(t, 1)
                scores(t, 0)
                scatter(2 * t - 2)
            scores(SLOT_TILES // 2 - 1, 1)
            for j in range(SLOT_TILES - 3, SLOT_TILES):
                scatter(j)
            pool.wait_ge(s_scatter, 16 * SLOT_TILES)

        @block.scalar
        def _(act_e):
            A = nc.scalar.activation

            for n in range(3 * HEADS * KT):
                act_e.wait_ge(s_wa, n + 1)
                A(qkvA[:, n // KT, n % KT, :], bank[n % 8][:, 0:A1], ACT.Copy).then_inc(s_wae, 1)
            for h in range(HEADS):
                act_e.wait_ge(s_gf, h + 1)
                A(GT[:, h, :], bank[h][:, 0:P], ACT.Copy)
                A(g_row[:, h:h + 1], bank[h][:, P:A1], ACT.Copy)
                A(g_col[:, h:h + 1], bank[h][:, 256:257], ACT.Copy)
                A(g00[0:1, h:h + 1], bank[h][0:1, 320:321], ACT.Copy).then_inc(s_gfe, 1)

            def F_hi(h):
                act_e.wait_ge(s_F, h + 1)
                A(F_hl[:, 0, h, :], bank[5 + h][:], ACT.Copy, scale=1.0 / HEADS).then_inc(w_Fh, 1)
            act_e.wait_ge(s_bload, 16 * 3)
            A(tokWT_hl[:, 0, :], tokWT_raw[:], ACT.Copy).then_inc(w_hi, 1)
            def patches_out(a):
                act_e.wait_ge(T["t_pt"], a + 1)
                A(PT[:], bank[0][:, 0:P], ACT.Copy)
                A(PT_hl[:, 0, :], bank[0][:, 0:P], ACT.Copy).then_inc(T["t_ptsb"], 1)

            act_e.wait_ge(s_f128, 1)
            A(g00_bc[:], bank[4][:, 0:HEADS], ACT.Copy)
            patches_out(0)
            A(tail_raw[0:HEADS, :], bank[3][0:HEADS, :], ACT.Copy, scale=1.0 / HEADS).then_inc(s_folded, 1)
            act_e.wait_ge(s_folded, 1)
            act_e.wait_ge(s_const, 1)
            A(tail[0:TAIL, :], tail_raw, ACT.Copy)
            A(tail[64:64 + TAIL, :], tail_raw, ACT.Copy).then_inc(w_hi, 1)
            F_hi(0)

            def token_tile(i, attend, ffn, more=True, looped=False, last=False):
                a, f = i + 1, i
                if ffn:
                    act_e.wait_ge(T["t_xtps"], f + 1)
                    for half, name in ((slice(0, KT // 2), "t_xta"), (slice(KT // 2, KT), "t_xtsb")):
                        A(xnT_hl[:, 0, half], bank[7][:].rearrange("p (k t) -> p k t", k=KT)[:, half],
                          ACT.Copy).then_inc(T[name], 1)
                if attend:
                    act_e.wait_ge(T["t_ups"], a + 1)
                    for h in range(HEADS):
                        ins = A(U[:, h, :], bank[1][:, h * P:(h + 1) * P], ACT.Identity, bias=g_col[:, h:h + 1])
                    ins.then_inc(T["t_usb"], 1)
                    if not ffn:
                        F_hi(1)
                if ffn:
                    act_e.wait_ge(T["t_xn"], f + 1)
                    act_e.wait_ge(T["t_acc"], f)
                    if not looped:
                        act_e.wait_ge(s_zrow, 32)
                    A(h2[:], bank[4][:], ACT.Copy).then_inc(T["t_h2sb"], 1)
                    act_e.wait_ge(s_raw, 16 * (f + 1))
                    act_e.wait_ge(s_cut, 16 * f)
                    A(blk_hl[:, 0, :], blk_raw, ACT.Copy).then_inc(c_hi, 1)
                if attend:
                    act_e.wait_ge(T["t_nmx"], a + 1)
                    for h in range(HEADS):
                        ins = A(ex[:, h, :], s1[:, h, :], ACT.Exp, bias=nmx[:, h:h + 1], scale=rscale[:, 0:1],
                                accum_out=esum[:, h:h + 1])
                    ins.then_inc(T["t_exp"], 1)
                    if not ffn:
                        F_hi(2)
                if ffn:
                    act_e.wait_ge(T["t_h1ps"], f + 1)
                    A(gate_t[:], bank[5][:, 0:HID], ACT.Tanh, scale=0.5).then_inc(T["t_tanh"], 1)
                if last:
                    act_e.wait_ge(r_ez, 1)
                    A(prob[:], z[:], ACT.Exp).then_inc(r_exp, 1)
                if attend:
                    act_e.wait_ge(T["t_yps"], a + 1)
                    A(YT_hl[:, 0], bank[3][:, 0:HEADS * P].rearrange("p (h t) -> p h t", h=HEADS),
                      ACT.Copy).then_inc(T["t_ysb"], 1)
                    act_e.wait_ge(T["t_y0ps"], a + 1)
                    for q in (0, 32):
                        ins = A(y0[q:q + HEADS, :], bank[1][0:HEADS, HEADS * P:(HEADS + 1) * P], ACT.Copy)
                    ins.then_inc(T["t_y0"], 1)
                if ffn:
                    act_e.wait_ge(T["t_htps"], f + 1)
                    A(hT_hl[:, 0], bank[2][:].rearrange("p (k t) -> p k t", k=KT), ACT.Copy).then_inc(T["t_htsb"], 1)
                if attend:
                    if more:
                        patches_out(a + 1)

            token_tile(-1, True, False)
            token_tile(0, True, True)
            with act_e.Fori(1, TILES - 2) as i:
                token_tile(i, True, True, looped=True)
            token_tile(TILES - 2, True, True, more=False)
            token_tile(TILES - 1, False, True, last=True)

            probf = prob_k[:].rearrange("p k t -> p (k t)")

            def hival_probs(g, b):
                act_e.wait_ge(r_oh, LB * g + b + 1)
                for c in range(CG):
                    ins = A(hival[b][:, c, SLOT_TILES:], hihot[b][:, c, :], ACT.Copy,
                            scale=probf[:, bass.ds((LB * g + b) * CG + c, 1)])
                ins.then_inc(r_hiprob, 1)

            for b in range(LB):
                hival_probs(0, b)
            with act_e.Fori(1, G) as g:
                for b in range(LB):
                    act_e.wait_ge(r_ohused, LB * (g - 1) + b + 1)
                    hival_probs(g, b)

            def x_out(j):
                act_e.wait_ge(R["e_xps"], j + 1)
                act_e.wait_ge(R["e_h3ps"], j)
                act_e.wait_ge(R["e_xlo"], j)
                A(xgT_hl[:, 0], bank[0][:].rearrange("p (k t) -> p k t", k=KT), ACT.Copy).then_inc(R["e_xsb"], 1)

            def silu(t, c):
                j = 2 * t + c
                act_e.wait_ge(R["e_h1ps"], j + 1)
                act_e.wait_ge(R["e_idx"], j + 1)
                act_e.wait_ge(R["e_act"], j)
                A(rgate[:], bank[1][:, 0:HID], ACT.Silu, scale=score[c][:, 0:1]).then_inc(R["e_gate"], 1)

            def h_out(j):
                act_e.wait_ge(R["e_htps"], j + 1)
                act_e.wait_ge(R["e_hlo"], j)
                A(rhT_hl[:, 0], bank[3][:].rearrange("p (k t) -> p k t", k=KT), ACT.Copy).then_inc(R["e_htsb"], 1)

            x_out(0)
            silu(0, 0)
            x_out(1)
            h_out(0)
            silu(0, 1)
            x_out(2)
            with act_e.Fori(1, SLOT_TILES // 2 - 1) as t:
                for c in range(2):
                    h_out(2 * t + c - 1)
                    silu(t, c)
                    x_out(2 * t + c + 1)
            h_out(SLOT_TILES - 3)
            silu(SLOT_TILES // 2 - 1, 0)
            x_out(SLOT_TILES - 1)
            h_out(SLOT_TILES - 2)
            silu(SLOT_TILES // 2 - 1, 1)
            h_out(SLOT_TILES - 1)

        @block.vector
        def _(dve):
            V = nc.vector
            n = [0]

            def link(ins):
                n[0] += 1
                ins.then_inc(s_dv, 1)
                dve.wait_ge(s_dv, n[0])

            dve.wait_ge(s_tok, 32)
            dve.wait_ge(s_mean, 1)
            link(V.tensor_copy(A_mean[:], bank[0][:, 0:A1]))
            link(V.tensor_tensor(A_T[:], A_T[:], A_mean[:].unsqueeze(1).broadcast_to([P, KT, A1]), ALU.subtract))
            V.tensor_tensor(bc2[:].unsqueeze(2), A_T[:, :, PATCH:A1], A_T[:, :, PATCH:A1], ALU.mult).then_inc(s_cen, 1)
            dve.wait_ge(s_sps, 1)
            V.tensor_scalar(S[:], bank[1][:, 0:A1], 1.0 / DIM, None, ALU.mult)
            V.tensor_scalar(s00e[:], bank[2][:, 0:1], EPS, None, ALU.add).then_inc(s_ssb, 1)
            dve.wait_ge(s_ssb, 1)
            dve.wait_ge(s_const, 1)
            dve.wait_ge(s_sw, 16)
            link(V.tensor_copy(shared[:, 0:SW_WORDS], sw_raw))
            V.tensor_tensor(shared[:, SW_WORDS:], sw_raw, shared[:, 0:SW_WORDS].bitcast(f32),
                            ALU.subtract).then_inc(w_lo, 1)
            dve.wait_ge(w_lo, 1)
            V.tensor_copy(sw2_hl[0][REST:P, FULL, :], sw2_hl[1][REST:P, FULL, :].bitcast(f32)).then_inc(w_lo, 1)

            def F_lo(h):
                dve.wait_ge(w_Fh, h + 1)
                V.scalar_tensor_tensor(out=F_hl[:, 1, h, :], in0=bank[5 + h][:], scalar=1.0 / HEADS,
                                       in1=part(F_hl, 0)[:, h, :], op0=ALU.mult, op1=ALU.subtract).then_inc(w_F, 1)
            dve.wait_ge(w_hi, 1)
            V.tensor_tensor(tokWT_hl[:, 1, :], tokWT_raw[:], part(tokWT_hl, 0), ALU.subtract).then_inc(w_lo, 1)

            def tail_lo():
                dve.wait_ge(w_hi, 2)
                V.tensor_tensor(tail[32:32 + TAIL, :], tail_raw, tail[0:TAIL, :].bitcast(f32),
                                ALU.subtract).then_inc(w_lo, 1)

            def add_stream(f, first=False):
                dve.wait_ge(T["t_ops"], f + 1)
                dve.wait_ge(T["t_h2sb"], f + 1)
                if not first:
                    dve.wait_ge(s_accst, 16 * f)
                V.tensor_tensor(acc[:], bank[6][:], h2[:], ALU.add).then_inc(T["t_acc"], 1)

            def bc(col):
                return col.unsqueeze(2).broadcast_to([P, TILES, EXPERTS])

            def routing_logits():
                dve.wait_ge(s_const, 2)
                dve.wait_ge(T["t_yps"], TILES)
                dve.wait_ge(T["t_h2ps"], TILES)
                dve.wait_ge(T["t_lg"], TILES)
                link(V.reduce_max(rmx[:], logits[:], axis=AX.X))
                V.tensor_tensor(z[:], logits[:], bc(rmx[:]), ALU.subtract).then_inc(r_ez, 1)

            def routing_probabilities():
                dve.wait_ge(r_exp, 1)
                link(V.reduce_sum(rsum[:], prob[:], axis=AX.X))
                link(V.reciprocal(rsum[:], rsum[:]))
                link(V.tensor_tensor(prob[:], prob[:], bc(rsum[:]), ALU.mult))
                dve.wait_ge(s_bias, 16)
                link(V.tensor_tensor(choice[:], prob[:], bias_bc[:].unsqueeze(1).broadcast_to([P, TILES, EXPERTS]),
                                     ALU.add))

            def best(v, i, oh, k):
                link(V.reduce_max(v[:], choice[:], axis=AX.X))
                link(V.tensor_tensor(eq[:], choice[:], bc(v[:]), ALU.is_ge))
                link(V.scalar_tensor_tensor(out=eq[:], in0=eq[:], scalar=-float(EXPERTS), in1=iota_e[:],
                                            op0=ALU.mult, op1=ALU.add))
                link(V.tensor_reduce(i[:], eq[:], axis=AX.X, op=ALU.min))
                link(V.tensor_scalar(i[:], i[:], float(EXPERTS), None, ALU.add))
                link(V.tensor_tensor(oh[:], iota_e[:], bc(i[:]), ALU.is_equal))

            def routing_choices():
                best(v1, i1, oh1, 0)
                link(V.scalar_tensor_tensor(out=choice[:], in0=oh1[:], scalar=-3.0e38, in1=choice[:],
                                            op0=ALU.mult, op1=ALU.add))
                best(v2, i2, oh2, 1)
                V.tensor_tensor(M[:], oh1[:], oh2[:], ALU.add).then_inc(r_M, 1)

            def token_tile(i, attend, ffn, before=True, first=False, last=False):
                a, f = i + 1, i

                def step(name, at, ins):
                    ins.then_inc(T[name], 1)
                    dve.wait_ge(T[name], at + 1)

                if attend:
                    dve.wait_ge(T["t_patch"], a + 1)
                    dve.wait_ge(T["t_sps"], a + 1)
                    V.tensor_tensor(c_sb[:], bank[0][:, P + A1:P + A1 + HEADS], g00_bc[:], ALU.add).then_inc(T["t_csb"], 1)
                    step("t_var", a, V.tensor_tensor_reduce(out=dots[:], in0=bank[0][:, P:P + A1], in1=patches[:],
                                                            scale=1.0, scalar=0.0, op0=ALU.mult, op1=ALU.add,
                                                            accum_out=varsum[:]))
                    V.tensor_scalar(varsum[:], varsum[:], s00e[:, 0:1], None, ALU.add).then_inc(T["t_vare"], 1)
                if not ffn:
                    tail_lo()
                    F_lo(0)
                if before:
                    add_stream(i - 1, first)
                if attend:
                    dve.wait_ge(T["t_rstd"], a + 1)
                    V.tensor_scalar(diag[:], ident[:], rstd[:, 0:1], None, ALU.mult).then_inc(T["t_diag"], 1)
                    V.tensor_scalar(rscale[:], rstd[:], float(DIM) ** -0.5, None, ALU.mult)
                    V.tensor_tensor(rmask[:], rstd[:], mask[:], ALU.mult).then_inc(T["t_rm"], 1)
                if ffn:
                    dve.wait_ge(T["t_xtsb"], f + 1)
                    V.tensor_tensor(xnT_hl[:, 1], bank[7][:].rearrange("p (k t) -> p k t", k=KT), part(xnT_hl, 0),
                                    ALU.subtract).then_inc(T["t_xlo"], 1)
                if attend:
                    dve.wait_ge(T["t_ptsb"], a + 1)
                    V.tensor_tensor(PT_hl[:, 1, :], PT[:], part(PT_hl, 0), ALU.subtract).then_inc(T["t_ptlo"], 1)
                    dve.wait_ge(T["t_rps"], a + 1)
                    V.tensor_copy(Rbc[:], bank[0][:, 448:448 + PAD_SEQ]).then_inc(T["t_rbc"], 1)
                    dve.wait_ge(T["t_csb"], a + 1)
                    dve.wait_ge(T["t_scps"], a + 1)
                    dve.wait_ge(T["t_rbc"], a + 1)
                    for h in range(HEADS):
                        ins = V.scalar_tensor_tensor(out=s1[:, h, :], in0=bank[2][:, h * PAD_SEQ:h * PAD_SEQ + SEQ],
                                                     scalar=c_sb[:, h:h + 1], in1=Rbc[:, 0:SEQ], op0=ALU.add,
                                                     op1=ALU.mult)
                    step("t_s1", a, ins)
                    step("t_mx", a, V.reduce_max(mx[:], s1[:], axis=AX.X))
                    dve.wait_ge(T["t_rm"], a + 1)
                    V.tensor_scalar(nmx[:], mx[:], rscale[:, 0:1], -1.0, ALU.mult, ALU.mult).then_inc(T["t_nmx"], 1)
                    if not ffn:
                        F_lo(1)
                if attend:
                    dve.wait_ge(T["t_exp"], a + 1)
                    step("t_esi", a, V.reciprocal(winv[:], esum[:]))
                    step("t_winv", a, V.tensor_scalar(winv[:], winv[:], rmask[:, 0:1], None, ALU.mult))
                    for half in range(2):
                        q = slice(half * PAD_SEQ, (half + 1) * PAD_SEQ)
                        ins = V.tensor_tensor(mixw[q, :, half * PAD_SEQ:half * PAD_SEQ + SEQ], ex[q],
                                              winv[q].unsqueeze(2).broadcast_to([PAD_SEQ, HEADS, SEQ]), ALU.mult)
                    ins.then_inc(T["t_mixw"], 1)
                    if not ffn:
                        F_lo(2)
                if ffn:
                    dve.wait_ge(T["t_tanh"], f + 1)
                    V.scalar_tensor_tensor(out=gate_t[:], in0=gate_t[:], scalar=1.0, in1=bank[5][:, 0:HID],
                                           op0=ALU.add, op1=ALU.mult).then_inc(T["t_sact"], 1)
                    V.tensor_copy(logits[:, bass.ds(f, 1), :].rearrange("p a e -> p (a e)"),
                                  bank[5][:, HID:GW]).then_inc(T["t_lg"], 1)
                if last:
                    routing_logits()
                if ffn:
                    dve.wait_ge(T["t_sact"], f + 1)
                    dve.wait_ge(T["t_h3ps"], f + 1)
                    V.scalar_tensor_tensor(out=act[:, HID:], in0=bank[6][:, FULL * P:HID], scalar=0.5,
                                           in1=gate_t[:, FULL * P:HID], op0=ALU.mult, op1=ALU.mult)
                    V.scalar_tensor_tensor(out=act[:, 0:HID], in0=bank[6][:, 0:HID], scalar=0.5, in1=gate_t[:],
                                           op0=ALU.mult, op1=ALU.mult).then_inc(T["t_act"], 1)
                if last:
                    routing_probabilities()
                if attend:
                    dve.wait_ge(T["t_ysb"], a + 1)
                    V.tensor_tensor(YT_hl[:, 1], bank[3][:, 0:HEADS * P].rearrange("p (h t) -> p h t", h=HEADS),
                                    part(YT_hl, 0), ALU.subtract)
                    dve.wait_ge(T["t_y0"], a + 1)
                    V.tensor_tensor(y0[64:64 + HEADS, :], bank[1][0:HEADS, HEADS * P:(HEADS + 1) * P],
                                    y0[0:HEADS, :].bitcast(f32), ALU.subtract).then_inc(T["t_ylo"], 1)
                if ffn:
                    dve.wait_ge(T["t_htsb"], f + 1)
                    V.tensor_tensor(hT_hl[:, 1], bank[2][:].rearrange("p (k t) -> p k t", k=KT),
                                    part(hT_hl, 0), ALU.subtract).then_inc(T["t_hlo"], 1)
                if attend:
                    dve.wait_ge(T["t_h2ps"], a + 1)
                    V.bn_stats(stats[:], bank[4][:]).then_inc(T["t_stats"], 1)
                    dve.wait_ge(s_const, 1)
                    dve.wait_ge(T["t_stats"], a + 1)
                    step("t_aggr", a, V.bn_aggr(aggr[:], stats[:]))
                    V.tensor_scalar(var2[:], aggr[:, 1:2], EPS, None, ALU.add).then_inc(T["t_var2"], 1)
                    dve.wait_ge(T["t_rstd2"], a + 1)
                    if ffn:
                        dve.wait_ge(s_xnst, 16 * a)
                    V.tensor_scalar(xn[:], bank[4][:], aggr[:, 0:1], rstd2[:, 0:1], ALU.subtract,
                                    ALU.mult).then_inc(T["t_xn"], 1)

            token_tile(-1, True, False, before=False)
            token_tile(0, True, True, before=False)
            token_tile(1, True, True, first=True)
            with dve.Fori(2, TILES - 1) as i:
                token_tile(i, True, True)
            token_tile(TILES - 1, False, True, last=True)
            routing_choices()
            add_stream(TILES - 1)
            for k, oh in enumerate((oh1, oh2)):
                link(V.tensor_tensor(tmp[:], oh[:], prob[:], ALU.mult))
                link(V.reduce_sum(prob_k[:, k, :], tmp[:], axis=AX.X))

            link(V.memset(z[:], 1.0))
            dve.wait_ge(r_rank, 1)
            rank_ps = bank[0][:, 0:TE].rearrange("p (t e) -> p t e", t=TILES)
            link(V.tensor_copy(tmp[:], bank[1][:, 0:TE].rearrange("p (t e) -> p t e", t=TILES)))
            for e in range(EXPERTS):
                last = V.tensor_tensor_scan(incl[:, :, e], z[:, :, e], tmp[:, :, e], 0.0, ALU.mult, ALU.add)
            link(last)
            link(V.tensor_scalar(totals[:], incl[:, TILES - 1, :], float(P - 1), None, ALU.add))
            link(V.tensor_copy(int_e[:], totals[:]))
            link(V.tensor_scalar(int_e[:], int_e[:], LOG_P, None, ALU.logical_shift_right))
            link(V.tensor_copy(ntiles[:], int_e[:]))
            link(V.tensor_scalar(ntiles[:], ntiles[:], 1.0, None, ALU.max))
            link(V.tensor_tensor_scan(ends[:], z[:, 0, :], ntiles[:], 0.0, ALU.mult, ALU.add))
            link(V.tensor_tensor(starts[:], ends[:], ntiles[:], ALU.subtract))
            link(V.tensor_tensor(incl[:], incl[:], tmp[:], ALU.subtract))
            link(V.tensor_tensor(incl[:], incl[:], rank_ps, ALU.add))
            link(V.scalar_tensor_tensor(out=pos[:], in0=starts[:].unsqueeze(1).broadcast_to([P, TILES, EXPERTS]),
                                        scalar=float(P), in1=incl[:], op0=ALU.mult, op1=ALU.add))
            for k, oh in enumerate((oh1, oh2)):
                link(V.tensor_tensor(tmp[:], oh[:], pos[:], ALU.mult))
                link(V.reduce_sum(pk[:, k, :], tmp[:], axis=AX.X))
            link(V.tensor_copy(int_k[:], pk[:]))
            link(V.tensor_scalar(int_low[:], int_k[:], P - 1, None, ALU.bitwise_and))
            link(V.tensor_copy(low[:], int_low[:]))
            link(V.tensor_scalar(int_k[:], int_k[:], LOG_P, None, ALU.logical_shift_right))
            link(V.tensor_copy(hi[:], int_k[:]))
            link(V.tensor_scalar(hi[:], hi[:], spare_off[:, 0:1], None, ALU.add))
            link(V.tensor_tensor(val[:], tok_id[:].unsqueeze(1).broadcast_to([P, TOPK, TILES]), low[:], ALU.subtract))
            link(V.tensor_scalar(val[:], val[:], -float(TOKENS), None, ALU.add))
            lowf, hif = (v[:].rearrange("p k t -> p (k t)") for v in (low, hi))

            def onehot_rows(g, b):
                cols = bass.ds((LB * g + b) * CG, CG)
                V.tensor_tensor(hihot[b][:], iota_s[:].unsqueeze(1).broadcast_to([P, CG, SLOT_TILES]),
                                hif[:, cols].unsqueeze(2).broadcast_to([P, CG, SLOT_TILES]),
                                ALU.is_equal)
                V.tensor_tensor(lowhot[b][:], iota_p[:].unsqueeze(1).broadcast_to([P, CG, P]),
                                lowf[:, cols].unsqueeze(2).broadcast_to([P, CG, P]), ALU.is_equal).then_inc(r_oh, 1)

            for b in range(LB):
                onehot_rows(0, b)
            with dve.Fori(1, G) as g:
                for b in range(LB):
                    dve.wait_ge(r_ohused, LB * (g - 1) + b + 1)
                    onehot_rows(g, b)
            link(V.tensor_tensor(te_cmp[:], iota_s[0:1, :].unsqueeze(2).broadcast_to([1, SLOT_TILES, EXPERTS]),
                                 ends[0:1, :].unsqueeze(1).broadcast_to([1, SLOT_TILES, EXPERTS]), ALU.is_ge))
            link(V.reduce_sum(te_sum[:], te_cmp[:], axis=AX.X))
            link(V.tensor_scalar(tile_expert[:], te_sum[:], float(EXPERTS - 1), None, ALU.min))
            link(V.tensor_scalar(te_place[:], te_sum[:], float(EXPERTS - 1), None, ALU.min))
            for m in range(RING_PLACES, EXPERTS, RING_PLACES):
                link(V.tensor_scalar(te_turn[:], te_sum[:], float(m), float(RING_PLACES), ALU.is_ge, ALU.mult))
                link(V.tensor_tensor(te_place[:], te_place[:], te_turn[:], ALU.subtract))
            link(V.tensor_copy(tile_place[:], te_place[:]))
            link(V.tensor_scalar(first_tile[:], starts[0:1, :], 1.0, None, ALU.add))

            dve.wait_ge(r_list, 1)
            V.tensor_scalar(slot_idx[:], bank[2][:, 0:SLOT_TILES], spare_row[:, 0:1], None, ALU.add)
            V.tensor_copy(slot_score[:], bank[2][:, SLOT_TILES:2 * SLOT_TILES]).then_inc(r_done, 1)

            def gate(t, c):
                j = 2 * t + c
                dve.wait_ge(R["e_gate"], j + 1)
                dve.wait_ge(R["e_h3ps"], j + 1)
                dve.wait_ge(R["e_htps"], j)
                V.scalar_tensor_tensor(out=ract[:, HID:], in0=bank[2][:, FULL * P:HID], scalar=score[c][:, 0:1],
                                       in1=rgate[:, FULL * P:HID], op0=ALU.mult, op1=ALU.mult)
                V.scalar_tensor_tensor(out=ract[:, 0:HID], in0=bank[2][:, 0:HID], scalar=score[c][:, 0:1], in1=rgate[:],
                                       op0=ALU.mult, op1=ALU.mult).then_inc(R["e_act"], 1)

            def y_out(j):
                dve.wait_ge(R["e_yps"], j + 2)
                dve.wait_ge(s_scatter, 16 * j)
                V.tensor_copy(y_sb[:], bank[4][:]).then_inc(R["e_ysb"], 1)

            def x_lo(j):
                dve.wait_ge(R["e_xsb"], j + 1)
                V.tensor_tensor(xgT_hl[:, 1], bank[0][:].rearrange("p (k t) -> p k t", k=KT), part(xgT_hl, 0),
                                ALU.subtract).then_inc(R["e_xlo"], 1)

            def h_lo(j):
                dve.wait_ge(R["e_htsb"], j + 1)
                V.tensor_tensor(rhT_hl[:, 1], bank[3][:].rearrange("p (k t) -> p k t", k=KT),
                                part(rhT_hl, 0), ALU.subtract).then_inc(R["e_hlo"], 1)

            x_lo(0)
            gate(0, 0)
            x_lo(1)
            h_lo(0)
            gate(0, 1)
            x_lo(2)
            y_out(0)
            with dve.Fori(1, SLOT_TILES // 2 - 1) as t:
                for c in range(2):
                    h_lo(2 * t + c - 1)
                    gate(t, c)
                    x_lo(2 * t + c + 1)
                    y_out(2 * t + c - 1)
            h_lo(SLOT_TILES - 3)
            gate(SLOT_TILES // 2 - 1, 0)
            x_lo(SLOT_TILES - 1)
            y_out(SLOT_TILES - 3)
            h_lo(SLOT_TILES - 2)
            gate(SLOT_TILES // 2 - 1, 1)
            y_out(SLOT_TILES - 2)
            h_lo(SLOT_TILES - 1)
            y_out(SLOT_TILES - 1)

        @block.tensor
        def _(pe):
            MM = nc.tensor.matmul

            pe.wait_ge(s_tok, 32)
            pe.wait_ge(s_ones, 1)
            for k in range(KT):
                ins = MM(bank[0][:, 0:A1], ones[:], A_T[:, k, :], start=k == 0, stop=k == KT - 1)
            ins.then_inc(s_mean, 1)
            pe.wait_ge(s_cen, 1)
            for k in range(KT):
                MM(bank[1][:, 0:A1], A_T[:, k, 0:P], A_T[:, k, :], start=k == 0, stop=k == KT - 1)
            for k in range(KT):
                ins = MM(bank[2][:, 0:1], ones[:], bc2[:, k:k + 1], start=k == 0, stop=k == KT - 1)
            ins.then_inc(s_sps, 1)
            pe.wait_ge(s_ssb, 1)
            for n in range(3 * HEADS * KT):
                m, db = n // KT, n % KT
                if db == 0:
                    pe.wait_ge(s_qkv[m], 16)
                if n >= 8:
                    pe.wait_ge(s_wae, n - 7)
                for k in range(KT):
                    ins = MM(bank[n % 8][:, 0:A1], qkvT[:, m, k, db * P:(db + 1) * P], A_T[:, k, :],
                             start=k == 0, stop=k == KT - 1)
                ins.then_inc(s_wa, 1)
            pe.wait_ge(s_wae, 3 * HEADS * KT)
            pe.wait_ge(s_fc, 16)
            for h in range(HEADS):
                QA, KA = qkvA[:, h], qkvA[:, HEADS + h]
                for dst, lhs, rhs in ((bank[h][:, 0:A1], KA[:, :, 0:P], QA[:, :, :]),
                                      (bank[h][:, 256:257], QA[:, :, 0:P], KA[:, :, P:A1]),
                                      (bank[h][0:1, 320:321], QA[:, :, P:A1], KA[:, :, P:A1])):
                    for k in range(KT):
                        ins = MM(dst, lhs[:, k, :], rhs[:, k, :], start=k == 0, stop=k == KT - 1)
                ins.then_inc(s_gf, 1)

            def product_F(h):
                for k in range(KT):
                    ins = MM(bank[5 + h][:], qkvA[:, 2 * HEADS + h, k, 0:P], fcT_sb[:, k, :],
                             start=k == 0, stop=k == KT - 1)
                ins.then_inc(s_F, 1)
            for k in range(KT):
                MM(bank[3][0:HEADS, :], qkvA[:, 2 * HEADS:3 * HEADS, k, P], fcT_sb[:, k, :],
                   start=k == 0, stop=k == KT - 1)
            pe.wait_ge(s_gfe, HEADS)
            pe.wait_ge(s_const, 1)
            MM(bank[4][:, 0:HEADS], ones_row[0:1, :], g00[0:1, :], start=True, stop=True).then_inc(s_f128, 1)

            def products(dst, pairs, lo_ready, start=True, stop=True, steps={}):
                for n, (x, w) in enumerate(pairs):
                    if n in steps:
                        steps[n]()
                    MM(dst, x[0], w[0], start=start and n == 0, stop=False)
                    MM(dst, x[0], w[1], start=False, stop=False)
                lo_ready()
                for n, (x, w) in enumerate(pairs):
                    ins = MM(dst, x[1], w[0], start=False, stop=stop and n == len(pairs) - 1)
                return ins

            def transpose_channels(dst, h):
                for k in range(FULL):
                    nc.tensor.transpose(dst[:, k * P:(k + 1) * P], h[:, k * P:(k + 1) * P], ident[:])
                return nc.tensor.transpose(dst[:, FULL * P:], h[:, FULL * P:], ident[:])

            def down_products(dst, hT, w2, lo_ready):
                for k in range(FULL):
                    for m in range(2):
                        MM(dst[:], hT[:, 0, k, :], w2(k, m), start=k == 0 and m == 0, stop=False)
                MM(dst[:], hT[:, 0, FULL, :], w2(FULL, 0), start=False, stop=False)
                lo_ready()
                for k in range(FULL):
                    MM(dst[:], hT[:, 1, k, :], w2(k, 0), start=False, stop=False)
                return MM(dst[:], hT[0:REST, 1, FULL, :], w2(FULL, 0)[0:REST], start=False, stop=True)

            def transpose_patches(a):
                pe.wait_ge(s_patch, 16 * a + 16)
                pe.wait_ge(T["t_rbc"], a)
                nc.tensor.transpose(bank[0][:, 0:P], next_patches, ident[:]).then_inc(T["t_pt"], 1)

            def y0_product(a, h):
                ins = MM(bank[1][0:HEADS, HEADS * P:(HEADS + 1) * P], onehot_h[:, h, :], mixw[:, h, :],
                         start=h == 0, stop=h == HEADS - 1)
                if h == HEADS - 1:
                    ins.then_inc(T["t_y0ps"], 1)

            def token_tile(i, attend, ffn, more=True):
                a, f = i + 1, i
                if attend:
                    pe.wait_ge(T["t_ptsb"], a + 1)
                    MM(bank[0][:, P:P + A1 + HEADS], PT[:], S_row[:], start=True, stop=True).then_inc(T["t_sps"], 1)
                if ffn:
                    pe.wait_ge(T["t_xn"], f + 1)
                    for k in range(KT):
                        ins = nc.tensor.transpose(bank[7][:, k * P:(k + 1) * P], xn[:, k * P:(k + 1) * P], ident[:])
                    ins.then_inc(T["t_xtps"], 1)
                if attend:
                    if ffn:
                        pe.wait_ge(T["t_ylo"], a)
                    for h in range(HEADS):
                        ins = MM(bank[1][:, h * P:(h + 1) * P], GT[:, h, :], PT[:], start=True, stop=True)
                    ins.then_inc(T["t_ups"], 1)
                    if not ffn:
                        product_F(1)

                def scores():
                    if attend:
                        pe.wait_ge(T["t_diag"], a + 1)
                        for half in range(2):
                            q = slice(half * PAD_SEQ, (half + 1) * PAD_SEQ)
                            ins = MM(bank[0][q, 448:448 + PAD_SEQ], ones1[:], diag[:, q], start=True, stop=True)
                        ins.then_inc(T["t_rps"], 1)
                        pe.wait_ge(T["t_usb"], a + 1)
                        if ffn:
                            pe.wait_ge(T["t_hlo"], f)
                        for h in range(HEADS):
                            for half in range(2):
                                q = slice(half * PAD_SEQ, (half + 1) * PAD_SEQ)
                                ins = MM(bank[2][q, h * PAD_SEQ:(h + 1) * PAD_SEQ], U[:, h, q], PT[:, q],
                                         start=True, stop=True)
                        ins.then_inc(T["t_scps"], 1)

                if ffn:
                    pe.wait_ge(T["t_xta"], f + 1)
                    pe.wait_ge(T["t_act"], f)
                    x_parts = [(xnT_hl[:, 0, k, :], xnT_hl[:, 1, k, :]) for k in range(KT)]
                    products(bank[5][:, 0:GW], [(x_parts[k], [w[:, k, :] for w in sw1g_hl]) for k in range(KT)],
                             lambda: pe.wait_ge(T["t_xlo"], f + 1),
                             steps={2: lambda: pe.wait_ge(T["t_xtsb"], f + 1), 3: scores}).then_inc(T["t_h1ps"], 1)
                    pe.wait_ge(T["t_acc"], f)
                    products(bank[6][:, 0:HID], [(x_parts[k], [w[:, k, :] for w in sw3_hl]) for k in range(KT)],
                             lambda: None).then_inc(T["t_h3ps"], 1)
                else:
                    scores()
                    product_F(2)
                if attend:
                    if not ffn:
                        pe.wait_ge(w_lo, 4)
                    pe.wait_ge(T["t_ptlo"], a + 1)
                    pe.wait_ge(T["t_h2sb"], a)
                    products(bank[4][:], [([PT_hl[:, n, :] for n in range(2)], [tokWT_hl[:, n, :] for n in range(2)])],
                             lambda: None, stop=False)
                    pe.wait_ge(T["t_mixw"], a + 1)
                    MM(bank[3][:, 0:HEADS * P], patches[:, 0:P], mixw[:].rearrange("p h t -> p (h t)"),
                       start=True, stop=True).then_inc(T["t_yps"], 1)
                    for h in range(HEADS):
                        y0_product(a, h)
                if ffn:
                    pe.wait_ge(T["t_act"], f + 1)
                    if attend:
                        pe.wait_ge(T["t_s1"], a + 1)
                    transpose_channels(bank[2], act).then_inc(T["t_htps"], 1)
                if attend:
                    if not ffn:
                        pe.wait_ge(w_F, HEADS)
                    pe.wait_ge(T["t_ysb"], a + 1)
                    products(bank[4][:], [([YT_hl[:, n, h, :] for n in range(2)], [F_hl[:, n, h, :] for n in range(2)])
                                          for h in range(HEADS)],
                             lambda: pe.wait_ge(T["t_ylo"], a + 1), start=False, stop=False)
                    MM(bank[4][:], y0[:], tail[:], start=False, stop=True).then_inc(T["t_h2ps"], 1)
                    if more:
                        transpose_patches(a + 1)
                if ffn:
                    pe.wait_ge(T["t_htsb"], f + 1)
                    down_products(bank[6], hT_hl, lambda k, m: sw2_hl[m][:, k, :],
                                  lambda: pe.wait_ge(T["t_hlo"], f + 1)).then_inc(T["t_ops"], 1)

            transpose_patches(0)
            product_F(0)
            token_tile(-1, True, False)
            token_tile(0, True, True)
            with pe.Fori(1, TILES - 2) as i:
                token_tile(i, True, True)
            token_tile(TILES - 2, True, True, more=False)
            token_tile(TILES - 1, False, True)

            pe.wait_ge(r_M, 1)
            Mf = M[:].rearrange("p t e -> p (t e)")
            MM(bank[0][:, 0:TE], tri[:], Mf, start=True, stop=True)
            MM(bank[1][:, 0:TE], mask[:, 0:1].broadcast_to([P, P]), Mf, start=True, stop=True).then_inc(r_rank, 1)

            def list_group(g, b, first, last):
                pe.wait_ge(r_hival, LB * g + b + 1)
                pe.wait_ge(r_hiprob, LB * g + b + 1)
                for c in range(CG):
                    ins = MM(bank[2][:, 0:2 * SLOT_TILES], lowhot[b][:, c, :], hival[b][:, c, :],
                             start=first and c == 0, stop=last and c == CG - 1)
                ins.then_inc(r_ohused, 1)
                return ins

            for b in range(LB):
                list_group(0, b, b == 0, False)
            with pe.Fori(1, G - 1) as g:
                for b in range(LB):
                    list_group(g, b, False, False)
            for b in range(LB):
                list_group(G - 1, b, False, b == LB - 1)
            nc.tensor.transpose(bank[3][:, 0:P], ident[:], ident[:]).then_inc(r_list, 1)
            pe.wait_ge(r_done, 1)

            def transpose_rows(t, c):
                j = 2 * t + c
                pe.wait_ge(s_gather[c], 16 * t + 16)
                pe.wait_ge(R["e_xlo"], j)
                for k in range(KT):
                    ins = nc.tensor.transpose(bank[0][:, k * P:(k + 1) * P], xg[c][:, k * P:(k + 1) * P], ident[:])
                ins.then_inc(R["e_xps"], 1)

            def weights(place, k, offset, n):
                o = place * PLACE + k * 2 * BLK + offset
                return [ring[:, bass.ds(o + m * BLK, n)] for m in range(2)]

            def up(j, place, offset, dst, done):
                products(dst[:, 0:HID], [([xgT_hl[:, n, k, :] for n in range(2)], weights(place, k, offset, HID))
                                         for k in range(KT)],
                         lambda: pe.wait_ge(R["e_xlo"], j + 1)).then_inc(done, 1)

            def transpose_hidden(j):
                pe.wait_ge(R["e_act"], j + 1)
                pe.wait_ge(R["e_hlo"], j)
                transpose_channels(bank[3], ract).then_inc(R["e_htps"], 1)

            def down(j, place):
                pe.wait_ge(R["e_htsb"], j + 1)
                pe.wait_ge(R["e_ysb"], j)
                down_products(bank[4], rhT_hl, lambda k, m: weights(place, k, 2 * HID, DIM)[m],
                              lambda: pe.wait_ge(R["e_hlo"], j + 1)).then_inc(R["e_yps"], 1)

            def place_of(j):
                return pe.value_load(tile_place[0:1, bass.ds(j, 1)], min_val=0, max_val=RING_PLACES - 1)

            def slot_tile(t, c, before=True, after=True):
                j = 2 * t + c
                e = pe.value_load(tile_expert[0:1, bass.ds(j, 1)], min_val=0, max_val=EXPERTS - 1)
                place = place_of(j)
                for b in range(2):
                    pe.wait_ge(s_expert[b], 16 * EXPERT_DMAS[b] * (e + 1))
                pe.wait_ge(R["e_xsb"], j + 1)
                if before:
                    pe.wait_ge(R["e_act"], j)
                up(j, place, 0, bank[1], R["e_h1ps"])
                if before:
                    transpose_hidden(j - 1)
                up(j, place, HID, bank[2], R["e_h3ps"])
                if after:
                    transpose_rows(t + c, 1 - c)
                if before:
                    down(j - 1, place_of(j - 1))

            nc.tensor.transpose(bank[4][:, 0:P], ident[:], ident[:]).then_inc(R["e_yps"], 1)
            transpose_rows(0, 0)
            slot_tile(0, 0, before=False)
            slot_tile(0, 1)
            with pe.Fori(1, SLOT_TILES // 2 - 1) as t:
                slot_tile(t, 0)
                slot_tile(t, 1)
            slot_tile(SLOT_TILES // 2 - 1, 0)
            slot_tile(SLOT_TILES // 2 - 1, 1, after=False)
            transpose_hidden(SLOT_TILES - 1)
            down(SLOT_TILES - 1, place_of(SLOT_TILES - 1))


def kernel(x, L0_tok_W, L0_tok_b, L0_attn_Wq, L0_attn_Wk, L0_attn_Wv, L0_attn_fc_w, L0_attn_fc_b, L0_ffn_gate_w,
           L0_ffn_w1, L0_ffn_w2, L0_ffn_w3, L0_ffn_sw1, L0_ffn_sw2, L0_ffn_sw3, L0_ffn_expert_bias):
    import numpy as np
    import concourse.bacc as bacc
    from concourse.bass_utils import run_bass_kernel_spmd

    def t(a):
        return np.ascontiguousarray(np.swapaxes(np.asarray(a), -1, -2))

    rows2 = np.minimum(np.arange(KT * P), FULL * P + np.arange(KT * P) % REST)
    w1, w2, w3 = (np.asarray(w) for w in (L0_ffn_w1, L0_ffn_w2, L0_ffn_w3))
    wpack = np.zeros((EXPERTS, KT, P, BLK), w1.dtype)
    wpack[..., 0:HID] = w1.reshape(EXPERTS, KT, P, HID)
    wpack[..., HID:2 * HID] = w3.reshape(EXPERTS, KT, P, HID)
    wpack[..., 2 * HID:] = w2[:, rows2].reshape(EXPERTS, KT, P, DIM)
    wpack = wpack.reshape(CHUNKS, P, BLK)
    swpack = np.zeros((P, KT * (GW + HID + DIM)), w1.dtype)
    up = swpack[:, 0:KT * GW].reshape(P, KT, GW)
    up[..., 0:HID] = np.asarray(L0_ffn_sw1).reshape(KT, P, HID).transpose(1, 0, 2)
    up[..., HID:] = np.asarray(L0_ffn_gate_w).reshape(KT, P, EXPERTS).transpose(1, 0, 2)
    swpack[:, 0:KT * GW] = up.reshape(P, KT * GW)
    swpack[:, KT * GW:KT * (GW + HID)] = np.asarray(L0_ffn_sw3).reshape(KT, P, HID).transpose(1, 0, 2).reshape(P, KT * HID)
    swpack[:, KT * (GW + HID):] = np.asarray(L0_ffn_sw2)[rows2].reshape(KT, P, DIM).transpose(1, 0, 2).reshape(P, KT * DIM)

    arrays = {
        "x": np.ascontiguousarray(np.asarray(x).reshape(-1)),
        "tokWT": t(L0_tok_W), "tokW": np.asarray(L0_tok_W), "tokb": np.asarray(L0_tok_b),
        "WqT": t(L0_attn_Wq), "WkT": t(L0_attn_Wk), "WvT": t(L0_attn_Wv), "fcT": t(L0_attn_fc_w),
        "fcb": np.asarray(L0_attn_fc_b),
        "wpack": wpack, "swpack": swpack,
        "ebias": np.asarray(L0_ffn_expert_bias),
    }
    nc = bacc.Bacc("TRN2", target_bir_lowering=False, num_devices=1)
    args = [nc.dram_tensor(f"in_{n}", a.shape, mybir.dt.from_np(a.dtype), kind="ExternalInput").ap()
            for n, a in arrays.items()]
    out = nc.dram_tensor("rows_out", (TOKENS + P, DIM), mybir.dt.float32, kind="ExternalOutput").ap()
    audio_tower(nc, *args, out)
    r = run_bass_kernel_spmd(nc, [{f"in_{n}": a for n, a in arrays.items()}], core_ids=[0])
    rows = r.results[0]["rows_out"]
    return rows[:TOKENS].reshape(BATCH, PAD_SEQ, DIM)[:, :SEQ]
```
